# Optimizing a Trainium2 kernel written in Bass

```python
import numpy as np
import jax
import jax.numpy as jnp

def _softmax(x, axis=-1):
    return jax.nn.softmax(x, axis=axis)

def _gelu(x):
    return jax.nn.gelu(x, approximate=True)

def _silu(x):
    return jax.nn.silu(x)

def _sigmoid(x):
    return jax.nn.sigmoid(x)

def _layernorm(x, axis=-1, eps=1e-05):
    m = jnp.mean(x, axis=axis, keepdims=True)
    v = jnp.var(x, axis=axis, keepdims=True)
    return (x - m) / jnp.sqrt(v + eps)

def _scatter_add(tgt, idx, src, axis=0):
    return tgt.at[idx].add(src)

def _segment_sum(src, seg, n):
    return jax.ops.segment_sum(src, seg, n)
kernel_name = 'mk_perceiver_d1_seqx_r4_37b7d8'

def setup_inputs(seed: int=0):
    np.random.seed(seed)
    _w = jnp.asarray

    def _rec_inputs():
        import jax
        import jax.numpy as jnp
        _rk = jax.random.key(seed)
        x = 7.22e-05 + 1 * jax.random.normal(jax.random.fold_in(_rk, 1), (4, 256, 256), jnp.float32)
        _lenS = 256 - jax.random.randint(jax.random.fold_in(_rk, 7), (4,), 0, max(1, 256 // 4) + 1, jnp.int32)
        _lenS2 = 4096 - jax.random.randint(jax.random.fold_in(_rk, 8), (4,), 0, max(1, 4096 // 4) + 1, jnp.int32)
        _ctx_1024P = jax.random.normal(jax.random.fold_in(_rk, 11), (4, 16, 256), jnp.float32)
        _ctx_1024c = jax.random.dirichlet(jax.random.fold_in(_rk, 511), 0.3 * jnp.ones((16,), jnp.float32), (4, 4096))
        _ctx_1024t = jnp.einsum('bsk,bkd->bsd', _ctx_1024c, _ctx_1024P)
        _ctx_1024t = _ctx_1024t * jax.lax.rsqrt(jnp.mean(jnp.square(_ctx_1024t)) + 1e-12) * 0.953939
        ctx_1024 = 4.13588e-05 + 0.999923 * (_ctx_1024t + 0.3 * jax.random.normal(jax.random.fold_in(_rk, 611), (4, 4096, 256), jnp.float32))
        return (x, ctx_1024)
    x, ctx_1024 = _rec_inputs()

    def _L0_xattn_setup():
        import jax, jax.numpy as jnp
        import numpy as np
        D_MODEL = 256
        HEADS = 16
        D_K = D_MODEL // HEADS
        SCALE = 1.0 / np.sqrt(D_K)

        def _proj(x, W, b):
            B, S, _ = x.shape
            return (x @ W + b).reshape(B, S, HEADS, D_K)
        key = jax.random.key(seed)
        ks = jax.random.split(key, 12)
        B, S = (4, 512)
        std = 1.0 / np.sqrt(D_MODEL)
        inp = {'query': jax.random.normal(ks[0], (B, S, D_MODEL), jnp.float32), 'key': jax.random.normal(ks[1], (B, S, D_MODEL), jnp.float32), 'value': jax.random.normal(ks[2], (B, S, D_MODEL), jnp.float32), 'Wq': jax.random.normal(ks[3], (D_MODEL, D_MODEL), jnp.float32) * std, 'bq': jax.random.normal(ks[4], (D_MODEL,), jnp.float32) * std, 'Wk': jax.random.normal(ks[5], (D_MODEL, D_MODEL), jnp.float32) * std, 'bk': jax.random.normal(ks[6], (D_MODEL,), jnp.float32) * std, 'Wv': jax.random.normal(ks[7], (D_MODEL, D_MODEL), jnp.float32) * std, 'bv': jax.random.normal(ks[8], (D_MODEL,), jnp.float32) * std, 'Wo': jax.random.normal(ks[9], (D_MODEL, D_MODEL), jnp.float32) * std, 'bo': jax.random.normal(ks[10], (D_MODEL,), jnp.float32) * std}
        return inp
    _L0_xattn_all = _L0_xattn_setup()
    _L0_xattn_in = {k: v for k, v in _L0_xattn_all.items() if k in ('Wq', 'bq', 'Wk', 'bk', 'Wv', 'bv', 'Wo', 'bo')}
    del _L0_xattn_all

    def _L0_attn_setup():
        import jax, jax.numpy as jnp
        import numpy as np
        B, N, DIM, H, DH = (2, 512, 256, 16, 64)
        INNER = H * DH
        EPS = 1e-12
        MAX_LOG_SCALE = np.log(1.0 / 0.01)
        key = jax.random.key(seed)
        k1, k2, k3, k4 = jax.random.split(key, 4)
        x = jax.random.normal(k1, (B, N, DIM), dtype=jnp.float32)
        w_qkv = jax.random.normal(k2, (DIM, 3 * INNER), dtype=jnp.float32) * DIM ** (-0.5)
        w_out = jax.random.normal(k3, (INNER, DIM), dtype=jnp.float32) * INNER ** (-0.5)
        b_out = jax.random.normal(k4, (DIM,), dtype=jnp.float32) * 0.01
        logit_scale = jnp.full((H, 1, 1), jnp.log(10.0), dtype=jnp.float32)
        return {'x': x, 'w_qkv': w_qkv, 'w_out': w_out, 'b_out': b_out, 'logit_scale': logit_scale}
    _L0_attn_all = _L0_attn_setup()
    _L0_attn_in = {k: v for k, v in _L0_attn_all.items() if k in ('w_qkv', 'w_out', 'b_out', 'logit_scale')}
    del _L0_attn_all

    def _L0_ffn_setup():
        import jax, jax.numpy as jnp
        import numpy as np
        B, T, D, E = (4, 256, 256, 8)
        HD = 4 * D
        key = jax.random.key(seed)
        k1, k2, k3, k4 = jax.random.split(key, 4)
        std = 0.5 * D ** (-0.5)
        bound = 3.0 ** 0.5 * std
        x = jax.random.normal(k1, (B, T, D), dtype=jnp.float32)
        router_w = jax.random.normal(k2, (E, D), dtype=jnp.float32) * 0.02
        expert_fc = jax.random.uniform(k3, (E, D, HD), dtype=jnp.float32, minval=-bound, maxval=bound)
        expert_proj = jax.random.normal(k4, (E, D, HD), dtype=jnp.float32) * 0.02
        return {'x': x, 'router_w': router_w, 'expert_fc': expert_fc, 'expert_proj': expert_proj}
    _L0_ffn_all = _L0_ffn_setup()
    _L0_ffn_in = {k: v for k, v in _L0_ffn_all.items() if k in ('router_w', 'expert_fc', 'expert_proj')}
    del _L0_ffn_all
    return {'x': x, 'ctx_1024': ctx_1024, 'L0_xattn_Wq': _L0_xattn_in['Wq'], 'L0_xattn_bq': _L0_xattn_in['bq'], 'L0_xattn_Wk': _L0_xattn_in['Wk'], 'L0_xattn_bk': _L0_xattn_in['bk'], 'L0_xattn_Wv': _L0_xattn_in['Wv'], 'L0_xattn_bv': _L0_xattn_in['bv'], 'L0_xattn_Wo': _L0_xattn_in['Wo'], 'L0_xattn_bo': _L0_xattn_in['bo'], 'L0_attn_w_qkv': _L0_attn_in['w_qkv'], 'L0_attn_w_out': _L0_attn_in['w_out'], 'L0_attn_b_out': _L0_attn_in['b_out'], 'L0_attn_logit_scale': _L0_attn_in['logit_scale'], 'L0_ffn_router_w': _L0_ffn_in['router_w'], 'L0_ffn_expert_fc': _L0_ffn_in['expert_fc'], 'L0_ffn_expert_proj': _L0_ffn_in['expert_proj']}

def reference(x, ctx_1024, L0_xattn_Wq, L0_xattn_bq, L0_xattn_Wk, L0_xattn_bk, L0_xattn_Wv, L0_xattn_bv, L0_xattn_Wo, L0_xattn_bo, L0_attn_w_qkv, L0_attn_w_out, L0_attn_b_out, L0_attn_logit_scale, L0_ffn_router_w, L0_ffn_expert_fc, L0_ffn_expert_proj):
    import jax
    import jax.numpy as jnp

    def _L0_xattn_ref(query, key, value, Wq, bq, Wk, bk, Wv, bv, Wo, bo):
        import jax, jax.numpy as jnp
        import numpy as np
        D_MODEL = 256
        HEADS = 16
        D_K = D_MODEL // HEADS
        SCALE = 1.0 / np.sqrt(D_K)

        def _proj(x, W, b):
            B, S, _ = x.shape
            return (x @ W + b).reshape(B, S, HEADS, D_K)
        B, S, _ = query.shape
        Q = _proj(query, Wq, bq)
        K = _proj(key, Wk, bk)
        V = _proj(value, Wv, bv)
        scores = jnp.einsum('bihd,bjhd->bijh', Q, K) * SCALE
        attn = jax.nn.softmax(scores, axis=1)
        x = jnp.einsum('bijh,bjhd->bihd', attn, V).reshape(B, S, D_MODEL)
        return x @ Wo + bo

    def _L0_attn_ref(x, w_qkv, w_out, b_out, logit_scale):
        import jax, jax.numpy as jnp
        import numpy as np
        B, N, DIM, H, DH = (2, 512, 256, 16, 64)
        INNER = H * DH
        EPS = 1e-12
        MAX_LOG_SCALE = np.log(1.0 / 0.01)
        b, n, dim = x.shape
        h = logit_scale.shape[0]
        qkv = x @ w_qkv
        q, k, v = jnp.split(qkv, 3, axis=-1)
        split_heads = lambda t: t.reshape(b, n, h, -1).transpose(0, 2, 1, 3)
        q, k, v = (split_heads(q), split_heads(k), split_heads(v))
        qn = q / jnp.maximum(jnp.linalg.norm(q, axis=-1, keepdims=True), EPS)
        kn = k / jnp.maximum(jnp.linalg.norm(k, axis=-1, keepdims=True), EPS)
        scale = jnp.exp(jnp.minimum(logit_scale, MAX_LOG_SCALE))
        cos_dots = jnp.einsum('bhid,bhjd->bhij', qn, kn) * scale
        attn = jax.nn.softmax(cos_dots, axis=-1)
        out = jnp.einsum('bhij,bhjd->bhid', attn, v)
        out = out.transpose(0, 2, 1, 3).reshape(b, n, -1)
        return out @ w_out + b_out

    def _L0_ffn_ref(x, router_w, expert_fc, expert_proj):
        import jax, jax.numpy as jnp
        import numpy as np
        B, T, D, E = (4, 256, 256, 8)
        HD = 4 * D
        logits = jnp.einsum('btd,ed->bte', x, router_w)
        probs = jax.nn.softmax(logits, axis=-1)
        expert_ids = jnp.argmax(probs, axis=-1)
        mask = jax.nn.one_hot(expert_ids, E, dtype=x.dtype)
        h = jnp.einsum('btd,edh->ebth', x, expert_fc)
        h = jnp.square(jax.nn.relu(h))
        out_e = jnp.einsum('ebth,edh->ebtd', h, expert_proj)
        output = jnp.einsum('ebtd,bte->btd', out_e, mask)
        return output
    x = x + _L0_xattn_ref(_layernorm(x, axis=-1), ctx_1024, ctx_1024, L0_xattn_Wq, L0_xattn_bq, L0_xattn_Wk, L0_xattn_bk, L0_xattn_Wv, L0_xattn_bv, L0_xattn_Wo, L0_xattn_bo)
    x = x + _L0_attn_ref(_layernorm(x, axis=-1), L0_attn_w_qkv, L0_attn_w_out, L0_attn_b_out, L0_attn_logit_scale)
    x = x + _L0_ffn_ref(_layernorm(x, axis=-1), L0_ffn_router_w, L0_ffn_expert_fc, L0_ffn_expert_proj)
    return x

_drawn_inputs = setup_inputs


def setup_inputs(seed=0):
    import zlib

    import numpy as np

    out = dict(_drawn_inputs(seed))
    spreads = {'L0_attn_logit_scale': (2.3025851249694824, 0.6)}
    factors = {'L0_xattn_bq': 8.0,
     'L0_xattn_bo': 8.0,
     'L0_attn_b_out': 8.0,
     'L0_ffn_router_w': 2.911,
     'L0_ffn_expert_fc': 3.078,
     'L0_ffn_expert_proj': 2.83}
    for name, (base, spread) in spreads.items():
        noise = np.random.default_rng([zlib.crc32(name.encode()), seed]).standard_normal(out[name].shape)
        drawn = base * np.exp(spread * noise) if base else spread * noise
        out[name] = jnp.asarray(drawn.astype(out[name].dtype))
    for name, factor in factors.items():
        out[name] = (out[name] * factor).astype(out[name].dtype)
    return out
```

```python
from contextlib import ExitStack

import concourse.bass as bass
from concourse import mybir

F32 = mybir.dt.float32
BF16 = mybir.dt.bfloat16
ALU = mybir.AluOpType
ACT = mybir.ActivationFunctionType
AX = mybir.AxisListType

P = 128
B, T, D = 4, 256, 256
S = 4096
H = 16
DK = D // H
KT = D // P
TT = B * T // P
TB = T // P
EPS = 1e-5

CH = 512
NCH = B * S // CH
NB = S // CH // 2
JC = CH // P
MT = D // P
HM = H // MT
PARTS = 3
PAIRS = [(0, 0), (0, 1), (0, 2), (1, 0), (1, 1), (2, 0)]
KR = DK * len(PAIRS)
GH = 4
NG = H // GH
STEP_GROUPS = 2 * JC * NG
STEP_UNITS = 2 * STEP_GROUPS
SRING = 4
PRING = 2 * NG
PRODUCTS = MT * KT + JC * KT
ORDER = [("keys", 0, 0, 0), ("keys", 0, 0, 1)] + [("values", 0, j, k) for j in (0, 1) for k in range(KT)] \
    + [("keys", 1, 0, 0), ("keys", 1, 0, 1)] + [("values", 1, j, k) for j in (2, 3) for k in range(KT)]
AHEAD = 2

HS, DH = 16, 64
INNER = HS * DH
SR = 3
MAX_LOG_SCALE = 4.605170185988092
NORM_EPS = 1e-12

E, HD = 8, 4 * D
DP = 32


def layer_norm_vector(dve, nc, x, out, tmp, stat, n, step, root, base):
    mean, var, std, inv, corr = (stat[:, i, :] for i in range(5))
    k = [0]

    def link(ins):
        k[0] += 1
        ins.then_inc(step, 1)
        dve.wait_ge(step, base + k[0])

    def wide(a):
        return a.unsqueeze(2).to_broadcast([P, n, D])

    link(nc.vector.tensor_reduce(mean, x, AX.X, ALU.add))
    link(nc.vector.tensor_scalar(mean, mean, 1.0 / D, None, ALU.mult))
    link(nc.vector.tensor_tensor(out, x, wide(mean), ALU.subtract))
    link(nc.vector.tensor_tensor(tmp, out, out, ALU.mult))
    link(nc.vector.tensor_reduce(var, tmp, AX.X, ALU.add))
    nc.vector.tensor_scalar(var, var, 1.0 / D, EPS, ALU.mult, ALU.add).then_inc(step, 1)
    dve.wait_ge(root[0], root[1])
    k[0] += 1
    link(nc.vector.reciprocal(inv, std))
    link(nc.vector.tensor_tensor(corr, var, inv, ALU.mult))
    link(nc.vector.tensor_tensor(corr, corr, inv, ALU.mult))
    link(nc.vector.tensor_scalar(corr, corr, -0.5, 1.5, ALU.mult, ALU.add))
    link(nc.vector.tensor_tensor(inv, inv, corr, ALU.mult))
    link(nc.vector.tensor_tensor(out, out, wide(inv), ALU.mult))
    assert k[0] == LN_STEPS


LN_STEPS = 12
LN_VAR = 6


def prepare(nc, dram, sb):
    with ExitStack() as ctx:
        def buf(name, shape, dt=F32):
            return ctx.enter_context(nc.sbuf_tensor(name, shape, dt))

        def sem(name):
            return ctx.enter_context(nc.semaphore(name))

        xn = buf("xn", [P, TT, D])
        sq = buf("sq", [P, TT, D])
        stat = buf("stat", [P, 5, TT])
        xnT = buf("xnT", [P, KT, B * T])
        wq = buf("wq", [P, KT, D])
        bq = buf("bq", [P, MT])
        bo = buf("bo", [P, D])
        qf = buf("qf", [P, MT, B * T])
        qr = buf("qr", [P, MT, B * T])
        qp = buf("qp", [P, MT, PARTS, B * T], BF16)
        pt = ctx.enter_context(nc.psum_tensor("pt", [P, 4, 512], F32))
        pq = ctx.enter_context(nc.psum_tensor("pq", [P, 4, 512], F32))

        x_in, wq_in, bo_in = sem("x_in"), sem("wq_in"), sem("bo_in")
        ident_ready = sem("ident_ready")
        ln_step, ln_root = sem("ln_step"), sem("ln_root")
        turned, turned_out = sem("turned"), sem("turned_out")
        q_ready, q_split, q_sent = sem("q_ready"), sem("q_split"), sem("q_sent")

        block = ctx.enter_context(nc.Block())

        @block.sync
        def _(sp):
            sp.dma_start(sb["x"][:, :, :], dram["x"].rearrange("(t p) d -> p t d", p=P)).then_inc(x_in, 16)
            sp.dma_start(wq[:, :, :], dram["wq"]).then_inc(wq_in, 16)
            sp.dma_start(bq[:, :], dram["bq"]).then_inc(wq_in, 16)
            sp.dma_start(bo[:, :], dram["bo"]).then_inc(bo_in, 16)
            for m in range(MT):
                sp.wait_ge(q_split, m + 1)
                for r, (_, part) in enumerate(PAIRS):
                    sp.dma_start(sb["q"][DK * r:DK * (r + 1), HM * m:HM * (m + 1), :], qp[:, m, part, :])\
                        .then_inc(q_sent, 16)
            sp.wait_ge(q_sent, 16 * MT * len(PAIRS))

        @block.gpsimd
        def _(pool):
            nc.gpsimd.memset(sb["ident"][:, :], 0.0).then_inc(ident_ready, 1)
            pool.wait_ge(ident_ready, 1)
            nc.gpsimd.affine_select(out=sb["ident"][:, :], in_=sb["ident"][:, :], compare_op=ALU.not_equal,
                                    fill=1.0, base=0, pattern=[[-1, P]], channel_multiplier=1)\
                .then_inc(ident_ready, 1)

        @block.scalar
        def _(act):
            act.wait_ge(ln_step, LN_VAR)
            nc.scalar.activation(stat[:, 2, :], stat[:, 1, :], ACT.Sqrt).then_inc(ln_root, 1)
            for b in range(4):
                act.wait_ge(turned, b + 1)
                half, k = b % 2, b // 2
                nc.scalar.copy(xnT[:, k, 512 * half:512 * (half + 1)], pt[:, b, :]).then_inc(turned_out, 1)

        @block.tensor
        def _(pe):
            pe.wait_ge(ident_ready, 2)
            pe.wait_ge(ln_step, LN_STEPS)
            for b in range(4):
                half, k = b % 2, b // 2
                for i in range(4):
                    last = nc.tensor.transpose(pt[:, b, P * i:P * (i + 1)],
                                               xn[:, 4 * half + i, P * k:P * (k + 1)], sb["ident"][:, :])
                last.then_inc(turned, 1)
            pe.wait_ge(wq_in, 32)
            pe.wait_ge(turned_out, 4)
            for m in range(MT):
                for half in range(2):
                    for k in range(KT):
                        last = nc.tensor.matmul(pq[:, 2 * m + half, :], wq[:, k, P * m:P * (m + 1)],
                                                xnT[:, k, 512 * half:512 * (half + 1)],
                                                start=(k == 0), stop=(k == KT - 1))
                    last.then_inc(q_ready, 1)

        @block.vector
        def _(dve):
            dve.wait_ge(x_in, 16)
            layer_norm_vector(dve, nc, sb["x"][:, :, :], xn[:, :, :], sq[:, :, :], stat, TT, ln_step, (ln_root, 1), 0)
            dve.wait_ge(bo_in, 16)
            nc.vector.tensor_tensor(sb["x"][:, :, :], sb["x"][:, :, :],
                                    bo[:, :].unsqueeze(1).to_broadcast([P, TT, D]), ALU.add)
            dve.wait_ge(wq_in, 32)
            n = LN_STEPS
            for m in range(MT):
                for half in range(2):
                    c = slice(512 * half, 512 * (half + 1))
                    dve.wait_ge(q_ready, 2 * m + half + 1)
                    last = nc.vector.tensor_scalar(qf[:, m, c], pq[:, 2 * m + half, :], bq[:, m:m + 1], DK ** -0.5,
                                                   ALU.add, ALU.mult)
                last.then_inc(ln_step, 1)
                n += 1
                dve.wait_ge(ln_step, n)
                nc.vector.tensor_copy(qp[:, m, 0, :], qf[:, m, :]).then_inc(ln_step, 1)
                n += 1
                dve.wait_ge(ln_step, n)
                nc.vector.tensor_tensor(qr[:, m, :], qf[:, m, :], qp[:, m, 0, :], ALU.subtract).then_inc(ln_step, 1)
                n += 1
                dve.wait_ge(ln_step, n)
                nc.vector.tensor_copy(qp[:, m, 1, :], qr[:, m, :]).then_inc(ln_step, 1)
                n += 1
                dve.wait_ge(ln_step, n)
                nc.vector.tensor_tensor(qp[:, m, 2, :], qr[:, m, :], qp[:, m, 1, :], ALU.subtract).then_inc(q_split, 1)


def cross_attention(nc, dram, sb):
    with ExitStack() as ctx:
        def buf(name, shape, dt=F32):
            return ctx.enter_context(nc.sbuf_tensor(name, shape, dt))

        def sem(name):
            return ctx.enter_context(nc.semaphore(name))

        wk = buf("wk", [P, KT, D])
        wv = buf("wv", [P, KT, D])
        bk = buf("bk", [P, MT])
        bv = buf("bv", [P, D])
        wo = buf("wo", [P, NG, D])
        zero = buf("zero", [P, 512], BF16)
        cT = buf("cT", [P, 2, KT, CH])
        kf = buf("kf", [P, MT, CH])
        kr = buf("kr", [P, MT, CH])
        kp = buf("kp", [P, MT, PARTS, CH], BF16)
        ks = buf("ks", [KR, 2, H, CH], BF16)
        v = buf("v", [P, 2, JC, D])
        vs = buf("vs", [P, 2, H, DP])
        nmax = buf("nmax", [P, 2, H])
        total = buf("total", [P, 2, H])
        inv = buf("inv", [P, 2, H])
        pr = buf("pr", [P, 2, H, T])
        oT = buf("oT", [P, NG, T])
        ps = ctx.enter_context(nc.psum_tensor("ps", [P, SRING, 2, T], F32))
        po = ctx.enter_context(nc.psum_tensor("po", [P, NG, T], F32))
        pk = ctx.enter_context(nc.psum_tensor("pk", [P, CH], F32))
        pv = ctx.enter_context(nc.psum_tensor("pv", [P, 2, D], F32))

        w_in = sem("w_in")
        zeroed = sem("zeroed")
        ctx_in = [sem("ctx_in0"), sem("ctx_in1")]
        ctx_used = sem("ctx_used")
        k_ready = sem("k_ready")
        k_copied = sem("k_copied")
        k_part0 = sem("k_part0")
        k_rest0 = sem("k_rest0")
        k_part1 = sem("k_part1")
        k_parts = sem("k_parts")
        k_sent = [sem("k_sent0"), sem("k_sent1")]
        v_ready = sem("v_ready")
        v_copied = sem("v_copied")
        s_ready = sem("s_ready")
        max_ready = sem("max_ready")
        exp_done = sem("exp_done")
        inv_ready = sem("inv_ready")
        vs_ready = sem("vs_ready")
        pv_done = sem("pv_done")
        cleared = sem("cleared")
        o_ready = sem("o_ready")
        proj_ready = sem("proj_ready")
        x_ready = sem("x_ready")
        SENT = 16 * MT * len(PAIRS)

        block = ctx.enter_context(nc.Block())

        @block.sync
        def _(sp):
            def load(c, parity):
                sp.dma_start(cT[:, parity, :, :], dram["ctxT"][bass.ds(c, 1), :, :, :]).then_inc(ctx_in[parity], 16)

            def send(m, tile, parity):
                sp.wait_ge(k_parts, tile + 1)
                for r, (part, _) in enumerate(PAIRS):
                    sp.dma_start(ks[DK * r:DK * (r + 1), parity, HM * m:HM * (m + 1), :], kp[:, m, part, :])\
                        .then_inc(k_sent[parity], 16)

            load(0, 0)
            sp.dma_start(wk[:, :, :], dram["wk"]).then_inc(w_in, 16)
            sp.dma_start(bk[:, :], dram["bk"]).then_inc(w_in, 16)
            sp.dma_start(wv[:, :, :], dram["wv"]).then_inc(w_in, 16)
            sp.dma_start(bv[:, :], dram["bv"]).then_inc(w_in, 16)
            sp.dma_start(wo[:, :, :], dram["wo"]).then_inc(w_in, 16)
            load(1, 1)
            for m in range(MT):
                send(m, m, 0)
            sp.dma_start(sb["wqkv"][:, :, :], dram["wqkv"]).then_inc(sb["attn_in"], 16)
            sp.dma_start(sb["wout"][:, :, :], dram["wout"]).then_inc(sb["attn_in"], 16)
            with sp.Fori(0, NCH // 2) as n:
                with sp.If(n < NCH // 2 - 1):
                    sp.wait_ge(ctx_used, 2 * n + 1)
                    load(nc.s_assert_le(2 * n + 2, NCH - 1), 0)
                sp.wait_ge(s_ready, STEP_UNITS * n)
                for m in range(MT):
                    send(m, MT * (2 * n + 1) + m, 1)
                with sp.If(n < NCH // 2 - 1):
                    sp.wait_ge(ctx_used, 2 * n + 2)
                    load(nc.s_assert_le(2 * n + 3, NCH - 1), 1)
                    sp.wait_ge(s_ready, STEP_UNITS * n + STEP_UNITS // 2)
                    for m in range(MT):
                        send(m, MT * (2 * n + 2) + m, 0)

        @block.gpsimd
        def _(pool):
            nc.gpsimd.memset(vs[:, :, :, :], 0.0).then_inc(zeroed, 1)
            nc.gpsimd.memset(zero[:, :], 0.0).then_inc(zeroed, 1)
            pool.wait_ge(zeroed, 2)
            pool.sem_inc(vs_ready, JC)

            def rest0(m, tile):
                pool.wait_ge(k_part0, tile + 1)
                nc.gpsimd.tensor_tensor(kr[:, m, :], kf[:, m, :], kp[:, m, 0, :], ALU.subtract).then_inc(k_rest0, 1)

            def rest1(m, tile):
                pool.wait_ge(k_part1, tile + 1)
                nc.gpsimd.tensor_tensor(kp[:, m, 2, :], kr[:, m, :], kp[:, m, 1, :], ALU.subtract).then_inc(k_parts, 1)

            def scale_values(j, parity, slot):
                pool.wait_ge(inv_ready, j + 1)
                pool.wait_ge(pv_done, PRING + NG * (j - 1))
                nc.gpsimd.tensor_tensor(
                    vs[:, slot % 2, :, 0:DK], v[:, parity, slot % JC, :].rearrange("p (h d) -> p h d", d=DK),
                    inv[:, slot % 2, :].unsqueeze(2).to_broadcast([P, H, DK]), ALU.mult).then_inc(vs_ready, 1)

            for m in range(MT):
                rest0(m, m)
                rest1(m, m)
            with pool.Fori(0, NCH // 2) as n:
                for cc in range(2):
                    for jj in range(JC):
                        slot = JC * cc + jj
                        scale_values(2 * JC * n + slot, cc, slot)
                        if jj < MT and cc == 0:
                            rest0(jj, MT * (2 * n + 1) + jj)
                            rest1(jj, MT * (2 * n + 1) + jj)
                        if jj < MT and cc == 1:
                            with pool.If(n < NCH // 2 - 1):
                                rest0(jj, MT * (2 * n + 2) + jj)
                                rest1(jj, MT * (2 * n + 2) + jj)

        @block.scalar
        def _(act):
            act.sem_inc(exp_done, SRING)
            with act.Fori(0, NCH // 2) as n:
                for g in range(STEP_GROUPS):
                    act.wait_ge(pv_done, STEP_GROUPS * n + g + 1)
                    par, hg = g // NG % 2, g % NG
                    for half in range(2):
                        act.wait_ge(max_ready, STEP_UNITS * n + 2 * g + half + 1)
                        for i in range(2):
                            h = GH * hg + 2 * half + i
                            last = nc.scalar.activation(pr[:, par, h, :], ps[:, (2 * g + half) % SRING, i, :], ACT.Exp,
                                                        bias=nmax[:, par, h:h + 1], accum_out=total[:, par, h:h + 1])
                        last.then_inc(exp_done, 1)

        @block.tensor
        def _(pe):
            def project(c, parity, turn, owed, k):
                kind, m, jj, kt = ORDER[k]
                if k == 0:
                    pe.wait_ge(ctx_in[parity], 16 * (turn + 1))
                    pe.wait_ge(x_ready, owed)
                if kind == "keys":
                    if kt == 0:
                        pe.wait_ge(k_copied, MT * c + m + 1)
                    mm = nc.tensor.matmul(pk[:, :], wk[:, kt, P * m:P * (m + 1)], cT[:, parity, kt, :],
                                          start=(kt == 0), stop=(kt == KT - 1))
                    if kt == KT - 1:
                        mm.then_inc(k_ready, 1)
                else:
                    if kt == 0 and jj % 2 == 0:
                        pe.wait_ge(v_copied, JC // 2 * c + m + 1)
                    mm = nc.tensor.matmul(pv[:, jj % 2, :], cT[:, parity, kt, P * jj:P * (jj + 1)], wv[:, kt, :],
                                          start=(kt == 0), stop=(kt == KT - 1))
                    if kt == KT - 1 and jj % 2 == 1:
                        mm.then_inc(v_ready, 1)
                if k == PRODUCTS - 1:
                    pe.wait_ge(v_ready, JC // 2 * (c + 1))
                    pe.sem_inc(ctx_used, 1)

            def scores(unit, local, parity, q0):
                pe.wait_ge(exp_done, unit + 1)
                jt, hp = divmod(local, H // 2)
                for i in range(2):
                    h = 2 * hp + i
                    mm = nc.tensor.matmul(ps[:, local % SRING, i, :], ks[:, parity, h, P * (jt % JC):P * (jt % JC + 1)],
                                          sb["q"][:, h, bass.ds(q0, T)], start=(i == 0), stop=True,
                                          skip_group_check=True)
                mm.then_inc(s_ready, 1)

            def values(group, local):
                par, hg = local // NG % 2, local % NG
                for i in range(GH):
                    h = GH * hg + i
                    mm = nc.tensor.matmul(po[DP * i:DP * (i + 1), hg, :], vs[:, par, h, :], pr[:, par, h, :],
                                          start=False, stop=True, skip_group_check=True)
                mm.then_inc(pv_done, 1)

            pe.sem_inc(pv_done, PRING)
            pe.wait_ge(w_in, 16 * 5)
            for k in range(PRODUCTS):
                project(0, 0, 0, 0, k)
            pe.wait_ge(zeroed, 2)
            pe.wait_ge(k_sent[0], SENT)
            for u in range(2 * AHEAD):
                scores(u, u, 0, 0)
            with pe.Fori(0, B) as b:
                for i in range(GH):
                    for bank in range(2):
                        mm = nc.tensor.matmul(po[DP * i:DP * (i + 1), 2 * bank:2 * bank + 2, :], zero[:, 0:DP],
                                              zero[:, :], start=True, stop=True, skip_group_check=True)
                with pe.Fori(0, NB) as it:
                    n = b * NB + it
                    q0 = b * T
                    for s in range(AHEAD, STEP_GROUPS):
                        cc = s // (STEP_GROUPS // 2)
                        if s == STEP_GROUPS // 2:
                            pe.wait_ge(k_sent[1], SENT * (n + 1))
                        for half in range(2):
                            scores(STEP_UNITS * n + 2 * s + half, 2 * s + half, cc, q0)
                        k = s % (STEP_GROUPS // 2) - AHEAD
                        if 0 <= k < PRODUCTS:
                            if cc == 0:
                                project(2 * n + 1, 1, n, b, k)
                            else:
                                with pe.If(n < NCH // 2 - 1):
                                    project(2 * n + 2, 0, n + 1, b, k)
                        g = s - NG - 2
                        if g >= 0:
                            if g % NG == 0:
                                pe.wait_ge(vs_ready, JC + 2 * JC * n + g // NG + 1)
                            values(STEP_GROUPS * n + g, g)
                    with pe.If(n < NCH // 2 - 1):
                        pe.wait_ge(k_sent[0], SENT * (n + 2))
                        for u in range(2 * AHEAD):
                            scores(STEP_UNITS * (n + 1) + u, u, 0, nc.s_assert_le(((n + 1) // NB) * T, (B - 1) * T))
                    for g in range(STEP_GROUPS - NG - 2, STEP_GROUPS):
                        if g % NG == 0:
                            pe.wait_ge(vs_ready, JC + 2 * JC * n + g // NG + 1)
                        values(STEP_GROUPS * n + g, g)
                pe.wait_ge(o_ready, b + 1)
                pe.wait_ge(k_copied, (MT * 2 * NB) * (b + 1) + 1)
                for t in range(TB):
                    for g in range(NG):
                        mm = nc.tensor.matmul(pk[:, D * t:D * (t + 1)], oT[:, g, P * t:P * (t + 1)], wo[:, g, :],
                                              start=(g == 0), stop=(g == NG - 1), skip_group_check=True)
                mm.then_inc(proj_ready, 1)

        @block.vector
        def _(dve):
            def copy_keys(m, tile):
                dve.wait_ge(k_ready, tile + 1)
                nc.vector.tensor_scalar(kf[:, m, :], pk[:, :], bk[:, m:m + 1], None, ALU.add).then_inc(k_copied, 1)
                dve.wait_ge(k_copied, tile + 2)
                nc.vector.tensor_copy(kp[:, m, 0, :], kf[:, m, :]).then_inc(k_part0, 1)

            def second_part(m, tile):
                dve.wait_ge(k_rest0, tile + 1)
                nc.vector.tensor_copy(kp[:, m, 1, :], kr[:, m, :]).then_inc(k_part1, 1)

            def copy_values(parity, pair, j2):
                dve.wait_ge(v_ready, j2 + 1)
                nc.vector.tensor_tensor(v[:, parity, 2 * pair:2 * pair + 2, :], pv[:, :, :],
                                        bv[:, :].unsqueeze(1).to_broadcast([P, 2, D]), ALU.add).then_inc(v_copied, 1)

            def maximum(unit, local):
                dve.wait_ge(s_ready, unit + 1)
                jt, hp = divmod(local, H // 2)
                nc.vector.tensor_reduce(nmax[:, jt % 2, 2 * hp:2 * hp + 2], ps[:, local % SRING, :, :], AX.X, ALU.max,
                                        negate=True).then_inc(max_ready, 1)

            def invert(j, local):
                dve.wait_ge(exp_done, SRING + (H // 2) * (j + 1))
                dve.wait_ge(vs_ready, JC + j - 1)
                nc.vector.reciprocal(inv[:, local % 2, :], total[:, local % 2, :]).then_inc(inv_ready, 1)

            def side_work(k, c, parity, sent):
                if k == 3:
                    dve.wait_ge(k_sent[1 - parity], sent)
                if k in (3, 8):
                    copy_keys(k // 8, MT * c + k // 8)
                if k in (5, 10):
                    second_part(k // 10, MT * c + k // 10)
                if k in (6, 12):
                    copy_values(parity, k // 12, JC // 2 * c + k // 12)

            dve.sem_inc(k_copied, 1)
            dve.sem_inc(v_copied, 1)
            dve.wait_ge(w_in, 16 * 5)
            for m in range(MT):
                copy_keys(m, m)
                second_part(m, m)
                copy_values(0, m, m)
            for u in range(2 * AHEAD):
                maximum(u, u)
            with dve.Fori(0, B) as b:
                with dve.Fori(0, NB) as it:
                    n = b * NB + it
                    for s in range(AHEAD, STEP_GROUPS):
                        for half in range(2):
                            maximum(STEP_UNITS * n + 2 * s + half, 2 * s + half)
                        if s % NG == 1 and s > NG:
                            invert(2 * JC * n + s // NG - 1, s // NG - 1)
                        k = s % (STEP_GROUPS // 2) - AHEAD
                        if k in (3, 5, 6, 8, 10, 12):
                            if s < STEP_GROUPS // 2:
                                side_work(k, 2 * n + 1, 1, SENT * (n + 1))
                            else:
                                with dve.If(n < NCH // 2 - 1):
                                    side_work(k, 2 * n + 2, 0, SENT * (n + 1))
                    with dve.If(n < NCH // 2 - 1):
                        for u in range(2 * AHEAD):
                            maximum(STEP_UNITS * (n + 1) + u, u)
                    invert(2 * JC * n + 2 * JC - 1, 2 * JC - 1)
                dve.wait_ge(pv_done, PRING + STEP_GROUPS * NB * (b + 1))
                nc.vector.tensor_copy(oT[:, :, :], po[:, :, :]).then_inc(o_ready, 1)
                dve.wait_ge(proj_ready, b + 1)
                xt = sb["x"][:, bass.ds(TB * b, TB), :]
                nc.vector.tensor_tensor(xt, pk[:, :].rearrange("p (t d) -> p t d", d=D), xt, ALU.add)\
                    .then_inc(x_ready, 1)


def self_attention(nc, dram, sb):
    with ExitStack() as ctx:
        def buf(name, shape, dt=F32):
            return ctx.enter_context(nc.sbuf_tensor(name, shape, dt))

        def sem(name):
            return ctx.enter_context(nc.semaphore(name))

        wqkv, wout, ident = sb["wqkv"], sb["wout"], sb["ident"]
        bout = buf("bout", [P, D])
        logit = buf("logit", [P, 2, HS])
        scale = buf("scale", [P, HS])
        xn = buf("sxn", [P, TB, D])
        sq = buf("ssq", [P, TB, D])
        stat = buf("sstat", [P, 5, TB])
        xnT = buf("sxnT", [P, KT, T])
        qk = buf("qk", [P, TB, 2 * INNER])
        sqr = buf("sqr", [P, 2, 512])
        nst = buf("nst", [P, 4, TB, 2 * HS])
        vv = buf("vv", [P, TB, INNER])
        qkT = buf("qkT", [P, 2 * INNER // P, T])
        nmax = buf("snmax", [P, SR, TB])
        total = buf("stotal", [P, 2, TB])
        inv = buf("sinv", [P, 2, TB])
        pr = buf("spr", [P, 2, TB, T])
        pn = buf("spn", [P, 2, TB, T])
        pT = buf("spT", [P, 2, TB, T])
        aT = buf("aT", [P, INNER // P, T])
        bank = ctx.enter_context(nc.psum_tensor("bank", [P, 8, 512], F32))
        TURN, QKV, QT, SC, PT_, OUT = 0, 1, 5, 0, 3, 5
        PROJ = 7

        logit_in, bout_in = sem("logit_in"), sem("bout_in")
        scaled = sem("scaled")
        ln_step = sem("sln_step")
        root = sem("sroot")
        xt_ready, xt_copied = sem("xt_ready"), sem("xt_copied")
        qkv_ready = sem("qkv_ready")
        squared, qk_copied = sem("squared"), sem("qk_copied")
        summed = sem("summed")
        vv_copied = sem("vv_copied")
        normed = sem("normed")
        qt_ready = sem("qt_ready")
        qt_even, qt_odd = sem("qt_even"), sem("qt_odd")
        s_ready, max_ready, exp_done = sem("ss_ready"), sem("smax_ready"), sem("sexp_done")
        pn_ready, t_ready, t_copied = sem("pn_ready"), sem("t_ready"), sem("t_copied")
        normed_p = sem("normed_p")
        pv_done, o_copied = sem("spv_done"), sem("o_copied")
        out_ready, x_ready = sem("sout_ready"), sem("sx_ready")
        NQK = 2 * INNER // 512 * TB
        NV = INNER // 512 * TB
        VSTEPS = LN_STEPS + 7

        block = ctx.enter_context(nc.Block())

        @block.sync
        def _(sp):
            sp.dma_start(logit[:, 0, :], dram["logit"]).then_inc(logit_in, 16)
            sp.dma_start(bout[:, :], dram["bout"]).then_inc(bout_in, 16)

        @block.scalar
        def _(act):
            with act.Fori(0, B) as b:
                act.wait_ge(ln_step, VSTEPS * b + LN_VAR)
                nc.scalar.activation(stat[:, 2, :], stat[:, 1, :], ACT.Sqrt).then_inc(root, 1)
                act.wait_ge(xt_ready, b + 1)
                nc.scalar.copy(xnT[:, :, :], bank[:, TURN, :].rearrange("p (k t) -> p k t", k=KT)).then_inc(xt_copied, 1)
                for m in range(NQK):
                    c, t = divmod(m, TB)
                    act.wait_ge(qkv_ready, (NQK + NV) * b + m + 1)
                    if m >= 2:
                        act.wait_ge(summed, NQK * b + m - 1)
                    nc.scalar.activation(sqr[:, m % 2, :], bank[:, QKV + m % 4, :], ACT.Square).then_inc(squared, 1)
                    nc.scalar.copy(qk[:, t, 512 * c:512 * (c + 1)], bank[:, QKV + m % 4, :]).then_inc(qk_copied, 1)
                act.wait_ge(ln_step, VSTEPS * b + LN_STEPS + 1)
                nc.scalar.activation(nst[:, 1, :, :], nst[:, 0, :, :], ACT.Sqrt).then_inc(root, 1)
                for w in range(0, NQK, 2):
                    act.wait_ge(qt_ready, NQK * b + w + 1)
                    nc.scalar.copy(qkT[:, 2 * w:2 * w + 2, :],
                                   bank[:, QT + w % 3, :].rearrange("p (a t) -> p a t", a=2)).then_inc(qt_even, 1)
                for s in range(HS + 2):
                    if s < HS:
                        act.wait_ge(max_ready, HS * b + s + 1)
                        if s >= 2:
                            act.wait_ge(pn_ready, HS * b + s - 1)
                        for i in range(TB):
                            last = nc.scalar.activation(pr[:, s % 2, i, :], bank[:, SC + s % SR, T * i:T * (i + 1)],
                                                        ACT.Exp, bias=nmax[:, s % SR, i:i + 1],
                                                        accum_out=total[:, s % 2, i:i + 1])
                        last.then_inc(exp_done, 1)
                    if s >= 2:
                        h = s - 2
                        act.wait_ge(t_ready, HS * b + h + 1)
                        if h >= 2:
                            act.wait_ge(pv_done, HS * b + h - 1)
                        nc.scalar.copy(pT[:, h % 2, :, :],
                                       bank[:, PT_ + h % 2, :].rearrange("p (j i) -> p j i", j=TB)).then_inc(t_copied, 1)

        @block.tensor
        def _(pe):
            pe.wait_ge(sb["attn_in"], 32)
            with pe.Fori(0, B) as b:
                pe.wait_ge(ln_step, VSTEPS * b + LN_STEPS)
                for k in range(KT):
                    for t in range(TB):
                        mm = nc.tensor.transpose(bank[:, TURN, T * k + P * t:T * k + P * (t + 1)],
                                                 xn[:, t, P * k:P * (k + 1)], ident[:, :])
                mm.then_inc(xt_ready, 1)
                pe.wait_ge(xt_copied, b + 1)
                for m in range(NQK + NV):
                    c, t = divmod(m, TB)
                    if 4 <= m < NQK + 4:
                        pe.wait_ge(qk_copied, NQK * b + m - 3)
                    for k in range(KT):
                        mm = nc.tensor.matmul(bank[:, QKV + m % 4, :], xnT[:, k, P * t:P * (t + 1)],
                                              wqkv[:, k, 512 * c:512 * (c + 1)], start=(k == 0), stop=(k == KT - 1))
                    mm.then_inc(qkv_ready, 1)
                for w in range(NQK):
                    pe.wait_ge(normed, NQK * b + min(NQK, 2 * (w // 2) + 2))
                    if w >= 3:
                        if w % 2:
                            pe.wait_ge(qt_even, NQK // 2 * b + (w - 3) // 2 + 1)
                        else:
                            pe.wait_ge(qt_odd, NQK // 2 * b + (w - 3) // 2 + 1)
                    for a in range(2):
                        for t in range(TB):
                            mm = nc.tensor.transpose(bank[:, QT + w % 3, T * a + P * t:T * a + P * (t + 1)],
                                                     qk[:, t, P * (2 * w + a):P * (2 * w + a + 1)], ident[:, :])
                    mm.then_inc(qt_ready, 1)
                pe.wait_ge(qt_even, NQK // 2 * (b + 1))
                pe.wait_ge(qt_odd, NQK // 2 * (b + 1))
                pe.wait_ge(vv_copied, NV * (b + 1))
                for s in range(HS + 3):
                    if s < HS:
                        if s >= SR:
                            pe.wait_ge(exp_done, HS * b + s - SR + 1)
                        r = slice(DH * (s % 2), DH * (s % 2 + 1))
                        for i in range(TB):
                            mm = nc.tensor.matmul(bank[:, SC + s % SR, T * i:T * (i + 1)],
                                                  qkT[r, s // 2, P * i:P * (i + 1)], qkT[r, HS // 2 + s // 2, :],
                                                  start=True, stop=True, skip_group_check=True)
                        mm.then_inc(s_ready, 1)
                    if 2 <= s < HS + 2:
                        h = s - 2
                        pe.wait_ge(pn_ready, HS * b + h + 1)
                        if h >= 2:
                            pe.wait_ge(t_copied, HS * b + h - 1)
                        for j in range(TB):
                            for i in range(TB):
                                mm = nc.tensor.transpose(bank[:, PT_ + h % 2, T * j + P * i:T * j + P * (i + 1)],
                                                         pn[:, h % 2, i, P * j:P * (j + 1)], ident[:, :])
                        mm.then_inc(t_ready, 1)
                    if s >= 3:
                        h = s - 3
                        pe.wait_ge(t_copied, HS * b + h + 1)
                        if h % 2 == 0 and h >= 4:
                            pe.wait_ge(o_copied, HS // 2 * b + h // 2 - 1)
                        for j in range(TB):
                            mm = nc.tensor.matmul(bank[DH * (h % 2):DH * (h % 2 + 1), OUT + h // 2 % 2, 0:T],
                                                  vv[:, j, DH * h:DH * (h + 1)], pT[:, h % 2, j, :],
                                                  start=(j == 0), stop=(j == TB - 1), skip_group_check=True)
                        mm.then_inc(pv_done, 1)
                pe.wait_ge(o_copied, HS // 2 * (b + 1))
                for t in range(TB):
                    for k in range(INNER // P):
                        mm = nc.tensor.matmul(bank[:, PROJ, D * t:D * (t + 1)], aT[:, k, P * t:P * (t + 1)],
                                              wout[:, k, :], start=(k == 0), stop=(k == INNER // P - 1),
                                              skip_group_check=True)
                mm.then_inc(out_ready, 1)

        @block.vector
        def _(dve):
            dve.wait_ge(logit_in, 16)
            k = 0
            y, t = logit[:, 1, :], scale[:, :]
            steps = [lambda: nc.vector.tensor_scalar(y, logit[:, 0, :], MAX_LOG_SCALE, 1.0 / 64, ALU.min, ALU.mult),
                     lambda: nc.vector.tensor_scalar(t, y, 1.0 / 7, 1.0, ALU.mult, ALU.add)]
            for n in range(6, 0, -1):
                steps.append(lambda: nc.vector.tensor_tensor(t, t, y, ALU.mult))
                steps.append(lambda n=n: nc.vector.tensor_scalar(t, t, 1.0 / n, 1.0, ALU.mult, ALU.add))
            steps += [lambda: nc.vector.tensor_tensor(t, t, t, ALU.mult)] * 6
            for step in steps:
                k += 1
                step().then_inc(scaled, 1)
                dve.wait_ge(scaled, k)
            dve.wait_ge(bout_in, 16)

            with dve.Fori(0, B) as b:
                x = sb["x"][:, bass.ds(TB * b, TB), :]
                base = VSTEPS * b
                layer_norm_vector(dve, nc, x, xn[:, :, :], sq[:, :, :], stat, TB, ln_step, (root, 2 * b + 1), base)
                for m in range(NQK):
                    c, t = divmod(m, TB)
                    dve.wait_ge(squared, NQK * b + m + 1)
                    nc.vector.tensor_reduce(nst[:, 0, t, 8 * c:8 * (c + 1)],
                                            sqr[:, m % 2, :].rearrange("p (h d) -> p h d", d=DH),
                                            AX.X, ALU.add).then_inc(summed, 1)
                for m in range(NV):
                    c, t = divmod(m, TB)
                    dve.wait_ge(qkv_ready, (NQK + NV) * b + NQK + m + 1)
                    nc.vector.tensor_copy(vv[:, t, 512 * c:512 * (c + 1)], bank[:, QKV + (NQK + m) % 4, :])\
                        .then_inc(vv_copied, 1)
                ss, nrm, inn, cor = (nst[:, i, :, :] for i in range(4))
                dve.wait_ge(summed, NQK * (b + 1))
                nc.vector.tensor_scalar(ss, ss, NORM_EPS ** 2, None, ALU.max).then_inc(ln_step, 1)
                base = base + LN_STEPS + 1
                dve.wait_ge(root, 2 * b + 2)
                nc.vector.reciprocal(inn, nrm).then_inc(ln_step, 1)
                dve.wait_ge(ln_step, base + 1)
                nc.vector.tensor_tensor(cor, ss, inn, ALU.mult).then_inc(ln_step, 1)
                dve.wait_ge(ln_step, base + 2)
                nc.vector.tensor_tensor(cor, cor, inn, ALU.mult).then_inc(ln_step, 1)
                dve.wait_ge(ln_step, base + 3)
                nc.vector.tensor_scalar(cor, cor, -0.5, 1.5, ALU.mult, ALU.add).then_inc(ln_step, 1)
                dve.wait_ge(ln_step, base + 4)
                nc.vector.tensor_tensor(inn, inn, cor, ALU.mult).then_inc(ln_step, 1)
                dve.wait_ge(ln_step, base + 5)
                nc.vector.tensor_tensor(inn[:, :, 0:HS], inn[:, :, 0:HS],
                                        scale[:, :].unsqueeze(1).to_broadcast([P, TB, HS]), ALU.mult).then_inc(ln_step, 1)
                dve.wait_ge(ln_step, base + 6)
                dve.wait_ge(qk_copied, NQK * (b + 1))
                for m in range(NQK):
                    c, t = divmod(m, TB)
                    a = qk[:, t, 512 * c:512 * (c + 1)].rearrange("p (h d) -> p h d", d=DH)
                    nc.vector.tensor_tensor(a, a, inn[:, t, 8 * c:8 * (c + 1)].unsqueeze(2).to_broadcast([P, 8, DH]),
                                            ALU.mult).then_inc(normed, 1)
                for w in range(1, NQK, 2):
                    dve.wait_ge(qt_ready, NQK * b + w + 1)
                    nc.vector.tensor_copy(qkT[:, 2 * w:2 * w + 2, :],
                                          bank[:, QT + w % 3, :].rearrange("p (a t) -> p a t", a=2)).then_inc(qt_odd, 1)
                for s in range(HS + 4):
                    if s < HS:
                        dve.wait_ge(s_ready, HS * b + s + 1)
                        nc.vector.tensor_reduce(nmax[:, s % SR, :],
                                                bank[:, SC + s % SR, :].rearrange("p (i j) -> p i j", i=TB),
                                                AX.X, ALU.max, negate=True).then_inc(max_ready, 1)
                    if 1 <= s < HS + 1:
                        h = s - 1
                        dve.wait_ge(exp_done, HS * b + h + 1)
                        if h >= 2:
                            dve.wait_ge(t_ready, HS * b + h - 1)
                        nc.vector.reciprocal(inv[:, h % 2, :], total[:, h % 2, :]).then_inc(normed_p, 1)
                        dve.wait_ge(normed_p, HS * b + h + 1)
                        for i in range(TB):
                            last = nc.vector.tensor_scalar(pn[:, h % 2, i, :], pr[:, h % 2, i, :],
                                                           inv[:, h % 2, i:i + 1], None, ALU.mult)
                        last.then_inc(pn_ready, 1)
                    if s >= 4 and s % 2 == 0 or s == HS + 3:
                        g = (s - 4) // 2 if s % 2 == 0 else HS // 2 - 1
                        if s % 2 == 0 and g < HS // 2 - 1 or s == HS + 3:
                            dve.wait_ge(pv_done, HS * b + 2 * g + 2)
                            nc.vector.tensor_copy(aT[:, g, :], bank[:, OUT + g % 2, 0:T]).then_inc(o_copied, 1)
                dve.wait_ge(out_ready, b + 1)
                nc.vector.tensor_tensor(x, bank[:, PROJ, :].rearrange("p (t d) -> p t d", d=D), x, ALU.add)\
                    .then_inc(x_ready, 1)
                dve.wait_ge(x_ready, 2 * b + 1)
                nc.vector.tensor_tensor(x, x, bout[:, :].unsqueeze(1).to_broadcast([P, TB, D]), ALU.add)\
                    .then_inc(x_ready, 1)


def experts(nc, dram, sb):
    with ExitStack() as ctx:
        def buf(name, shape, dt=F32):
            return ctx.enter_context(nc.sbuf_tensor(name, shape, dt))

        def sem(name):
            return ctx.enter_context(nc.semaphore(name))

        ident = sb["ident"]
        xn = buf("exn", [P, TT, D])
        sq = buf("esq", [P, TT, D])
        stat = buf("estat", [P, 5, TT])
        xnT = buf("exnT", [P, KT, B * T])
        router = buf("router", [P, KT, E])
        lg = buf("lg", [P, TT, E])
        best = buf("best", [P, TT])
        rank = buf("rank", [P, E])
        mask = buf("mask", [P, TT, E])
        fc = buf("fc", [P, 2, KT, HD])
        pj = buf("pj", [P, 2, HD // P, D])
        rl = buf("rl", [P, 2, 512])
        hT = buf("hT", [P, 2, HD // P, 512])
        bank = ctx.enter_context(nc.psum_tensor("ebank", [P, 8, 512], F32))
        HR = 3
        HT = HD // P

        router_in = sem("router_in")
        fc_in, pj_in = [sem("fc_in0"), sem("fc_in1")], [sem("pj_in0"), sem("pj_in1")]
        ln_step, root = sem("eln_step"), sem("eroot")
        turned, turned_out = sem("eturned"), sem("eturned_out")
        ranked = sem("ranked")
        lg_ready, mask_step = sem("lg_ready"), sem("mask_step")
        h_ready = sem("h_ready")
        h_relu = sem("h_relu")
        h_done = sem("h_done")
        e_ready = sem("e_ready")
        e_added = sem("e_added")
        e_used = sem("e_used")
        NH = 2 * HT
        NO = TT // 2

        block = ctx.enter_context(nc.Block())

        @block.sync
        def _(sp):
            sp.dma_start(router[:, :, :], dram["router"]).then_inc(router_in, 16)
            with sp.Fori(0, E // 2) as n:
                for k in range(2):
                    sp.wait_ge(e_used, 2 * n + k)
                    sp.dma_start(fc[:, k, :, :], dram["fc"][bass.ds(2 * n + k, 1), :, :, :]).then_inc(fc_in[k], 16)
                    sp.dma_start(pj[:, k, :, :], dram["pj"][bass.ds(2 * n + k, 1), :, :, :]).then_inc(pj_in[k], 16)

        @block.gpsimd
        def _(pool):
            for e in range(E):
                nc.gpsimd.memset(rank[:, e:e + 1], float(E - e)).then_inc(ranked, 1)

        @block.scalar
        def _(act):
            act.wait_ge(ln_step, LN_VAR)
            nc.scalar.activation(stat[:, 2, :], stat[:, 1, :], ACT.Sqrt).then_inc(root, 1)
            for b in range(4):
                act.wait_ge(turned, b + 1)
                half, k = b % 2, b // 2
                nc.scalar.copy(xnT[:, k, 512 * half:512 * (half + 1)], bank[:, b, :]).then_inc(turned_out, 1)
            with act.Fori(0, E // 2) as n:
                for m in range(2 * NH):
                    act.wait_ge(h_ready, 2 * NH * n + m + 1)
                    act.wait_ge(h_done, 2 * NH * n + m + 2)
                    nc.scalar.activation(rl[:, m % 2, :], bank[:, m % 4, :], ACT.Relu).then_inc(h_relu, 1)

        @block.tensor
        def _(pe):
            pe.wait_ge(ln_step, LN_STEPS)
            for b in range(4):
                half, k = b % 2, b // 2
                for i in range(4):
                    last = nc.tensor.transpose(bank[:, b, P * i:P * (i + 1)],
                                               xn[:, 4 * half + i, P * k:P * (k + 1)], ident[:, :])
                last.then_inc(turned, 1)
            pe.wait_ge(router_in, 16)
            pe.wait_ge(turned_out, 4)
            for t in range(TT):
                for k in range(KT):
                    last = nc.tensor.matmul(bank[:, 7, E * t:E * (t + 1)], xnT[:, k, P * t:P * (t + 1)], router[:, k, :],
                                            start=(k == 0), stop=(k == KT - 1), skip_group_check=True)
            last.then_inc(lg_ready, 1)
            with pe.Fori(0, E // 2) as n:
                for ee in range(2):
                    pe.wait_ge(fc_in[ee], 16 * (n + 1))
                    for half in range(2):
                        for ht in range(HT):
                            m = NH * ee + HT * half + ht
                            pe.wait_ge(h_done, 2 * NH * n + m)
                            for k in range(KT):
                                mm = nc.tensor.matmul(bank[:, m % 4, :], fc[:, ee, k, P * ht:P * (ht + 1)],
                                                      xnT[:, k, 512 * half:512 * (half + 1)],
                                                      start=(k == 0), stop=(k == KT - 1))
                            mm.then_inc(h_ready, 1)
                    pe.wait_ge(pj_in[ee], 16 * (n + 1))
                    for o in range(NO):
                        half, o2 = divmod(o, 2)
                        if o2 == 0:
                            pe.wait_ge(h_done, 3 + 2 * NH * n + NH * ee + HT * (half + 1))
                        oo = NO * ee + o
                        pe.wait_ge(e_added, 2 * NO * n + oo + 1)
                        for i in range(2):
                            t = 2 * o2 + i
                            for ht in range(HT):
                                mm = nc.tensor.matmul(bank[:, 4 + oo % 4, D * i:D * (i + 1)],
                                                      hT[:, half, ht, P * t:P * (t + 1)], pj[:, ee, ht, :],
                                                      start=(ht == 0), stop=(ht == HT - 1), skip_group_check=True)
                        mm.then_inc(e_ready, 1)
                    pe.wait_ge(e_ready, 2 * NO * n + NO * (ee + 1))
                    pe.sem_inc(e_used, 1)

        @block.vector
        def _(dve):
            layer_norm_vector(dve, nc, sb["x"][:, :, :], xn[:, :, :], sq[:, :, :], stat, TT, ln_step, (root, 1), 0)
            dve.wait_ge(lg_ready, 1)
            dve.wait_ge(ranked, E)
            step = [0]

            def link(ins):
                step[0] += 1
                ins.then_inc(mask_step, 1)
                dve.wait_ge(mask_step, step[0])

            wide = [P, TT, E]
            link(nc.vector.tensor_copy(lg[:, :, :], bank[:, 7, 0:TT * E].rearrange("p (t e) -> p t e", e=E)))
            link(nc.vector.tensor_reduce(best[:, :], lg[:, :, :], AX.X, ALU.max))
            link(nc.vector.tensor_tensor(lg[:, :, :], lg[:, :, :], best[:, :].unsqueeze(2).to_broadcast(wide), ALU.is_equal))
            link(nc.vector.tensor_tensor(lg[:, :, :], lg[:, :, :], rank[:, :].unsqueeze(1).to_broadcast(wide), ALU.mult))
            link(nc.vector.tensor_reduce(best[:, :], lg[:, :, :], AX.X, ALU.max))
            link(nc.vector.tensor_tensor(mask[:, :, :], lg[:, :, :], best[:, :].unsqueeze(2).to_broadcast(wide), ALU.is_equal))
            dve.sem_inc(h_done, 3)
            dve.sem_inc(e_added, 4)
            with dve.Fori(0, E // 2) as n:
                for ee in range(2):
                    for k in range(NH):
                        m = NH * ee + k
                        half, ht = divmod(k, HT)
                        dve.wait_ge(h_relu, 2 * NH * n + m + 1)
                        if ht == 0:
                            dve.wait_ge(e_ready, 2 * NO * n + NO * ee)
                        nc.vector.tensor_tensor(hT[:, half, ht, :], rl[:, m % 2, :], rl[:, m % 2, :], ALU.mult)\
                            .then_inc(h_done, 1)
                    for o in range(NO):
                        oo = NO * ee + o
                        dve.wait_ge(e_ready, 2 * NO * n + oo + 1)
                        for i in range(2):
                            t = 2 * o + i
                            xt = sb["x"][:, t, :]
                            last = nc.vector.scalar_tensor_tensor(xt, bank[:, 4 + oo % 4, D * i:D * (i + 1)],
                                                                  mask[:, t, bass.ds(2 * n + ee, 1)], xt,
                                                                  ALU.mult, ALU.add)
                        last.then_inc(e_added, 1)


def finish(nc, dram, sb):
    with ExitStack() as ctx:
        out_sent = ctx.enter_context(nc.semaphore("out_sent"))
        block = ctx.enter_context(nc.Block())

        @block.sync
        def _(sp):
            sp.dma_start(dram["out"].rearrange("(t p) d -> p t d", p=P), sb["x"][:, :, :]).then_inc(out_sent, 16)
            sp.wait_ge(out_sent, 16)


def program(nc, dram):
    with ExitStack() as ctx:
        def buf(name, shape, dt=F32):
            return ctx.enter_context(nc.sbuf_tensor(name, shape, dt))

        sb = {
            "x": buf("x", [P, TT, D]),
            "ident": buf("ident", [P, P]),
        }
        sb["attn_in"] = ctx.enter_context(nc.semaphore("attn_in"))
        with nc.sbuf_tensor("wqkv", [P, KT, 3 * INNER], F32) as sb["wqkv"], \
                nc.sbuf_tensor("wout", [P, INNER // P, D], F32) as sb["wout"]:
            with nc.sbuf_tensor("q_stacked", [KR, H, B * T], BF16) as sb["q"]:
                prepare(nc, dram, sb)
                cross_attention(nc, dram, sb)
            self_attention(nc, dram, sb)
        experts(nc, dram, sb)
        finish(nc, dram, sb)


def kernel(x, ctx_1024, L0_xattn_Wq, L0_xattn_bq, L0_xattn_Wk, L0_xattn_bk, L0_xattn_Wv, L0_xattn_bv, L0_xattn_Wo,
           L0_xattn_bo, L0_attn_w_qkv, L0_attn_w_out, L0_attn_b_out, L0_attn_logit_scale, L0_ffn_router_w,
           L0_ffn_expert_fc, L0_ffn_expert_proj):
    import numpy as np
    import concourse.bacc as bacc
    from concourse.bass_utils import run_bass_kernel_spmd

    def rows(w):
        w = np.asarray(w)
        return w.reshape(w.shape[0] // P, P, -1).transpose(1, 0, 2)

    def by_width(w):
        w = np.asarray(w)
        return w.reshape(-1, MT, HM, DK).transpose(0, 1, 3, 2).reshape(-1, D)

    def every(v):
        return np.broadcast_to(np.asarray(v).reshape(1, -1), (P, np.asarray(v).size))

    wo = np.zeros((NG, GH, DP, D), np.float32)
    wo[:, :, :DK, :] = np.asarray(L0_xattn_Wo).reshape(NG, GH, DK, D)
    arrays = {
        "x": np.asarray(x).reshape(B * T, D),
        "ctxT": np.asarray(ctx_1024).reshape(NCH, CH, KT, P).transpose(0, 3, 2, 1),
        "wq": rows(by_width(L0_xattn_Wq)),
        "bq": by_width(np.asarray(L0_xattn_bq)[None]).reshape(MT, P).T,
        "wk": rows(by_width(L0_xattn_Wk)),
        "bk": by_width(np.asarray(L0_xattn_bk)[None]).reshape(MT, P).T,
        "wv": rows(L0_xattn_Wv),
        "bv": every(L0_xattn_bv),
        "wo": wo.reshape(NG, P, D).transpose(1, 0, 2),
        "bo": every(L0_xattn_bo),
        "wqkv": rows(L0_attn_w_qkv),
        "wout": rows(L0_attn_w_out),
        "bout": every(L0_attn_b_out),
        "logit": every(L0_attn_logit_scale),
        "router": rows(np.asarray(L0_ffn_router_w).T),
        "fc": np.asarray(L0_ffn_expert_fc).reshape(E, KT, P, HD).transpose(0, 2, 1, 3),
        "pj": np.asarray(L0_ffn_expert_proj).reshape(E, D, HD // P, P).transpose(0, 3, 2, 1),
    }
    nc = bacc.Bacc("TRN2", target_bir_lowering=False, num_devices=1)
    dram = {}
    for name, a in arrays.items():
        arrays[name] = a = np.ascontiguousarray(a)
        dram[name] = nc.dram_tensor(f"{name}_dram", a.shape, mybir.dt.from_np(a.dtype), kind="ExternalInput").ap()
    dram["out"] = nc.dram_tensor("out_dram", (B * T, D), F32, kind="ExternalOutput").ap()
    program(nc, dram)
    r = run_bass_kernel_spmd(nc, [{f"{k}_dram": a for k, a in arrays.items()}], core_ids=[0])
    return r.results[0]["out_dram"].reshape(B, T, D)
```

```python
from contextlib import ExitStack

import concourse.bass as bass
from concourse import mybir

F32 = mybir.dt.float32
BF16 = mybir.dt.bfloat16
ALU = mybir.AluOpType
ACT = mybir.ActivationFunctionType
AX = mybir.AxisListType

P = 128
B, T, D = 4, 256, 256
S = 4096
H = 16
DK = D // H
KT = D // P
TT = B * T // P
TB = T // P
EPS = 1e-5

CH = 512
NCH = B * S // CH
NB = S // CH // 2
JC = CH // P
MT = D // P
HM = H // MT
PARTS = 3
PAIRS = [(0, 0), (0, 1), (0, 2), (1, 0), (1, 1), (2, 0)]
KR = DK * len(PAIRS)
GH = 4
NG = H // GH
STEP_GROUPS = 2 * JC * NG
STEP_UNITS = 2 * STEP_GROUPS
SRING = 4
PRING = 2 * NG
PRODUCTS = MT * KT + JC * KT
ORDER = [("keys", 0, 0, 0), ("keys", 0, 0, 1)] + [("values", 0, j, k) for j in (0, 1) for k in range(KT)] \
    + [("keys", 1, 0, 0), ("keys", 1, 0, 1)] + [("values", 1, j, k) for j in (2, 3) for k in range(KT)]
AHEAD = 2

HS, DH = 16, 64
INNER = HS * DH
SR = 3
MAX_LOG_SCALE = 4.605170185988092
NORM_EPS = 1e-12

E, HD = 8, 4 * D
SLOT_TILES = TT + E - 1
DP = 32


def layer_norm_vector(dve, nc, x, out, tmp, stat, n, step, root, base):
    mean, var, std, inv, corr = (stat[:, i, :] for i in range(5))
    k = [0]

    def link(ins):
        k[0] += 1
        ins.then_inc(step, 1)
        dve.wait_ge(step, base + k[0])

    def wide(a):
        return a.unsqueeze(2).to_broadcast([P, n, D])

    link(nc.vector.tensor_reduce(mean, x, AX.X, ALU.add))
    link(nc.vector.tensor_scalar(mean, mean, 1.0 / D, None, ALU.mult))
    link(nc.vector.tensor_tensor(out, x, wide(mean), ALU.subtract))
    link(nc.vector.tensor_tensor(tmp, out, out, ALU.mult))
    link(nc.vector.tensor_reduce(var, tmp, AX.X, ALU.add))
    nc.vector.tensor_scalar(var, var, 1.0 / D, EPS, ALU.mult, ALU.add).then_inc(step, 1)
    dve.wait_ge(root[0], root[1])
    k[0] += 1
    link(nc.vector.reciprocal(inv, std))
    link(nc.vector.tensor_tensor(corr, var, inv, ALU.mult))
    link(nc.vector.tensor_tensor(corr, corr, inv, ALU.mult))
    link(nc.vector.tensor_scalar(corr, corr, -0.5, 1.5, ALU.mult, ALU.add))
    link(nc.vector.tensor_tensor(inv, inv, corr, ALU.mult))
    link(nc.vector.tensor_tensor(out, out, wide(inv), ALU.mult))
    assert k[0] == LN_STEPS


LN_STEPS = 12
LN_VAR = 6


def prepare(nc, dram, sb):
    with ExitStack() as ctx:
        def buf(name, shape, dt=F32):
            return ctx.enter_context(nc.sbuf_tensor(name, shape, dt))

        def sem(name):
            return ctx.enter_context(nc.semaphore(name))

        xn = buf("xn", [P, TT, D])
        sq = buf("sq", [P, TT, D])
        stat = buf("stat", [P, 5, TT])
        xnT = buf("xnT", [P, KT, B * T])
        wq = buf("wq", [P, KT, D])
        bq = buf("bq", [P, MT])
        bo = buf("bo", [P, D])
        qf = buf("qf", [P, MT, B * T])
        qr = buf("qr", [P, MT, B * T])
        qp = buf("qp", [P, MT, PARTS, B * T], BF16)
        zrow = buf("zrow", [P, 3, D])
        zeroed = sem("rows_zeroed")
        pt = ctx.enter_context(nc.psum_tensor("pt", [P, 4, 512], F32))
        pq = ctx.enter_context(nc.psum_tensor("pq", [P, 4, 512], F32))

        x_in, wq_in, bo_in = sem("x_in"), sem("wq_in"), sem("bo_in")
        ident_ready = sem("ident_ready")
        ln_step, ln_root = sem("ln_step"), sem("ln_root")
        turned, turned_out = sem("turned"), sem("turned_out")
        q_ready, q_split, q_sent = sem("q_ready"), sem("q_split"), sem("q_sent")

        block = ctx.enter_context(nc.Block())

        @block.sync
        def _(sp):
            sp.dma_start(sb["x"][:, :, :], dram["x"].rearrange("(t p) d -> p t d", p=P)).then_inc(x_in, 16)
            sp.dma_start(wq[:, :, :], dram["wq"]).then_inc(wq_in, 16)
            sp.dma_start(bq[:, :], dram["bq"]).then_inc(wq_in, 16)
            sp.dma_start(bo[:, :], dram["bo"]).then_inc(bo_in, 16)
            sp.wait_ge(zeroed, 1)
            for t in range(0, SLOT_TILES, 3):
                sp.dma_start(dram["sorted_x"][t:t + 3].rearrange("t p d -> p t d"), zrow[:, :, :])\
                    .then_inc(sb["zeroed_rows"], 16)
            sp.wait_ge(sb["zeroed_rows"], 16 * (SLOT_TILES // 3))
            for m in range(MT):
                sp.wait_ge(q_split, m + 1)
                for r, (_, part) in enumerate(PAIRS):
                    sp.dma_start(sb["q"][DK * r:DK * (r + 1), HM * m:HM * (m + 1), :], qp[:, m, part, :])\
                        .then_inc(q_sent, 16)
            sp.wait_ge(q_sent, 16 * MT * len(PAIRS))

        @block.gpsimd
        def _(pool):
            nc.gpsimd.memset(zrow[:, :, :], 0.0).then_inc(zeroed, 1)
            nc.gpsimd.memset(sb["ident"][:, :], 0.0).then_inc(ident_ready, 1)
            pool.wait_ge(ident_ready, 1)
            nc.gpsimd.affine_select(out=sb["ident"][:, :], in_=sb["ident"][:, :], compare_op=ALU.not_equal,
                                    fill=1.0, base=0, pattern=[[-1, P]], channel_multiplier=1)\
                .then_inc(ident_ready, 1)

        @block.scalar
        def _(act):
            act.wait_ge(ln_step, LN_VAR)
            nc.scalar.activation(stat[:, 2, :], stat[:, 1, :], ACT.Sqrt).then_inc(ln_root, 1)
            for b in range(4):
                act.wait_ge(turned, b + 1)
                half, k = b % 2, b // 2
                nc.scalar.copy(xnT[:, k, 512 * half:512 * (half + 1)], pt[:, b, :]).then_inc(turned_out, 1)

        @block.tensor
        def _(pe):
            pe.wait_ge(ident_ready, 2)
            pe.wait_ge(ln_step, LN_STEPS)
            for b in range(4):
                half, k = b % 2, b // 2
                for i in range(4):
                    last = nc.tensor.transpose(pt[:, b, P * i:P * (i + 1)],
                                               xn[:, 4 * half + i, P * k:P * (k + 1)], sb["ident"][:, :])
                last.then_inc(turned, 1)
            pe.wait_ge(wq_in, 32)
            pe.wait_ge(turned_out, 4)
            for m in range(MT):
                for half in range(2):
                    for k in range(KT):
                        last = nc.tensor.matmul(pq[:, 2 * m + half, :], wq[:, k, P * m:P * (m + 1)],
                                                xnT[:, k, 512 * half:512 * (half + 1)],
                                                start=(k == 0), stop=(k == KT - 1))
                    last.then_inc(q_ready, 1)

        @block.vector
        def _(dve):
            dve.wait_ge(x_in, 16)
            layer_norm_vector(dve, nc, sb["x"][:, :, :], xn[:, :, :], sq[:, :, :], stat, TT, ln_step, (ln_root, 1), 0)
            dve.wait_ge(bo_in, 16)
            nc.vector.tensor_tensor(sb["x"][:, :, :], sb["x"][:, :, :],
                                    bo[:, :].unsqueeze(1).to_broadcast([P, TT, D]), ALU.add)
            dve.wait_ge(wq_in, 32)
            n = LN_STEPS
            for m in range(MT):
                for half in range(2):
                    c = slice(512 * half, 512 * (half + 1))
                    dve.wait_ge(q_ready, 2 * m + half + 1)
                    last = nc.vector.tensor_scalar(qf[:, m, c], pq[:, 2 * m + half, :], bq[:, m:m + 1], DK ** -0.5,
                                                   ALU.add, ALU.mult)
                last.then_inc(ln_step, 1)
                n += 1
                dve.wait_ge(ln_step, n)
                nc.vector.tensor_copy(qp[:, m, 0, :], qf[:, m, :]).then_inc(ln_step, 1)
                n += 1
                dve.wait_ge(ln_step, n)
                nc.vector.tensor_tensor(qr[:, m, :], qf[:, m, :], qp[:, m, 0, :], ALU.subtract).then_inc(ln_step, 1)
                n += 1
                dve.wait_ge(ln_step, n)
                nc.vector.tensor_copy(qp[:, m, 1, :], qr[:, m, :]).then_inc(ln_step, 1)
                n += 1
                dve.wait_ge(ln_step, n)
                nc.vector.tensor_tensor(qp[:, m, 2, :], qr[:, m, :], qp[:, m, 1, :], ALU.subtract).then_inc(q_split, 1)


def cross_attention(nc, dram, sb):
    with ExitStack() as ctx:
        def buf(name, shape, dt=F32):
            return ctx.enter_context(nc.sbuf_tensor(name, shape, dt))

        def sem(name):
            return ctx.enter_context(nc.semaphore(name))

        wk = buf("wk", [P, KT, D])
        wv = buf("wv", [P, KT, D])
        bk = buf("bk", [P, MT])
        bv = buf("bv", [P, D])
        wo = buf("wo", [P, NG, D])
        zero = buf("zero", [P, 512], BF16)
        cT = buf("cT", [P, 2, KT, CH])
        kf = buf("kf", [P, MT, CH])
        kr = buf("kr", [P, MT, CH])
        kp = buf("kp", [P, MT, PARTS, CH], BF16)
        ks = buf("ks", [KR, 2, H, CH], BF16)
        v = buf("v", [P, 2, JC, D])
        vs = buf("vs", [P, 2, H, DP])
        nmax = buf("nmax", [P, 2, H])
        total = buf("total", [P, 2, H])
        inv = buf("inv", [P, 2, H])
        pr = buf("pr", [P, 2, H, T])
        oT = buf("oT", [P, NG, T])
        ps = ctx.enter_context(nc.psum_tensor("ps", [P, SRING, 2, T], F32))
        po = ctx.enter_context(nc.psum_tensor("po", [P, NG, T], F32))
        pk = ctx.enter_context(nc.psum_tensor("pk", [P, CH], F32))
        pv = ctx.enter_context(nc.psum_tensor("pv", [P, 2, D], F32))

        w_in = sem("w_in")
        zeroed = sem("zeroed")
        ctx_in = [sem("ctx_in0"), sem("ctx_in1")]
        ctx_used = sem("ctx_used")
        k_ready = sem("k_ready")
        k_copied = sem("k_copied")
        k_part0 = sem("k_part0")
        k_rest0 = sem("k_rest0")
        k_part1 = sem("k_part1")
        k_parts = sem("k_parts")
        k_sent = [sem("k_sent0"), sem("k_sent1")]
        v_ready = sem("v_ready")
        v_copied = sem("v_copied")
        s_ready = sem("s_ready")
        max_ready = sem("max_ready")
        exp_done = sem("exp_done")
        inv_ready = sem("inv_ready")
        vs_ready = sem("vs_ready")
        pv_done = sem("pv_done")
        cleared = sem("cleared")
        o_ready = sem("o_ready")
        proj_ready = sem("proj_ready")
        x_ready = sem("x_ready")
        SENT = 16 * MT * len(PAIRS)

        block = ctx.enter_context(nc.Block())

        @block.sync
        def _(sp):
            def load(c, parity):
                sp.dma_start(cT[:, parity, :, :], dram["ctxT"][bass.ds(c, 1), :, :, :]).then_inc(ctx_in[parity], 16)

            def send(m, tile, parity):
                sp.wait_ge(k_parts, tile + 1)
                for r, (part, _) in enumerate(PAIRS):
                    sp.dma_start(ks[DK * r:DK * (r + 1), parity, HM * m:HM * (m + 1), :], kp[:, m, part, :])\
                        .then_inc(k_sent[parity], 16)

            load(0, 0)
            sp.dma_start(wk[:, :, :], dram["wk"]).then_inc(w_in, 16)
            sp.dma_start(bk[:, :], dram["bk"]).then_inc(w_in, 16)
            sp.dma_start(wv[:, :, :], dram["wv"]).then_inc(w_in, 16)
            sp.dma_start(bv[:, :], dram["bv"]).then_inc(w_in, 16)
            sp.dma_start(wo[:, :, :], dram["wo"]).then_inc(w_in, 16)
            load(1, 1)
            for m in range(MT):
                send(m, m, 0)
            sp.dma_start(sb["wqkv"][:, :, :], dram["wqkv"]).then_inc(sb["attn_in"], 16)
            sp.dma_start(sb["wout"][:, :, :], dram["wout"]).then_inc(sb["attn_in"], 16)
            with sp.Fori(0, NCH // 2) as n:
                with sp.If(n < NCH // 2 - 1):
                    sp.wait_ge(ctx_used, 2 * n + 1)
                    load(nc.s_assert_le(2 * n + 2, NCH - 1), 0)
                sp.wait_ge(s_ready, STEP_UNITS * n + 1)
                for m in range(MT):
                    send(m, MT * (2 * n + 1) + m, 1)
                with sp.If(n < NCH // 2 - 1):
                    sp.wait_ge(ctx_used, 2 * n + 2)
                    load(nc.s_assert_le(2 * n + 3, NCH - 1), 1)
                    sp.wait_ge(s_ready, STEP_UNITS * n + STEP_UNITS // 2)
                    for m in range(MT):
                        send(m, MT * (2 * n + 2) + m, 0)

        @block.gpsimd
        def _(pool):
            nc.gpsimd.memset(vs[:, :, :, :], 0.0).then_inc(zeroed, 1)
            nc.gpsimd.memset(zero[:, :], 0.0).then_inc(zeroed, 1)
            pool.wait_ge(zeroed, 2)
            pool.sem_inc(vs_ready, JC)

            def rest0(m, tile):
                pool.wait_ge(k_part0, tile + 1)
                nc.gpsimd.tensor_tensor(kr[:, m, :], kf[:, m, :], kp[:, m, 0, :], ALU.subtract).then_inc(k_rest0, 1)

            def rest1(m, tile):
                pool.wait_ge(k_part1, tile + 1)
                nc.gpsimd.tensor_tensor(kp[:, m, 2, :], kr[:, m, :], kp[:, m, 1, :], ALU.subtract).then_inc(k_parts, 1)

            def scale_values(j, parity, slot):
                pool.wait_ge(inv_ready, j + 1)
                pool.wait_ge(pv_done, PRING + NG * (j - 1))
                nc.gpsimd.tensor_tensor(
                    vs[:, slot % 2, :, 0:DK], v[:, parity, slot % JC, :].rearrange("p (h d) -> p h d", d=DK),
                    inv[:, slot % 2, :].unsqueeze(2).to_broadcast([P, H, DK]), ALU.mult).then_inc(vs_ready, 1)

            for m in range(MT):
                rest0(m, m)
                rest1(m, m)
            with pool.Fori(0, NCH // 2) as n:
                for cc in range(2):
                    for jj in range(JC):
                        slot = JC * cc + jj
                        scale_values(2 * JC * n + slot, cc, slot)
                        if jj < MT and cc == 0:
                            rest0(jj, MT * (2 * n + 1) + jj)
                            rest1(jj, MT * (2 * n + 1) + jj)
                        if jj < MT and cc == 1:
                            with pool.If(n < NCH // 2 - 1):
                                rest0(jj, MT * (2 * n + 2) + jj)
                                rest1(jj, MT * (2 * n + 2) + jj)

        @block.scalar
        def _(act):
            act.sem_inc(exp_done, SRING)
            with act.Fori(0, NCH // 2) as n:
                for g in range(STEP_GROUPS):
                    act.wait_ge(pv_done, STEP_GROUPS * n + g + 1)
                    par, hg = g // NG % 2, g % NG
                    for half in range(2):
                        act.wait_ge(max_ready, STEP_UNITS * n + 2 * g + half + 1)
                        for i in range(2):
                            h = GH * hg + 2 * half + i
                            last = nc.scalar.activation(pr[:, par, h, :], ps[:, (2 * g + half) % SRING, i, :], ACT.Exp,
                                                        bias=nmax[:, par, h:h + 1], accum_out=total[:, par, h:h + 1])
                        last.then_inc(exp_done, 1)

        @block.tensor
        def _(pe):
            def project(c, parity, turn, owed, k):
                kind, m, jj, kt = ORDER[k]
                if k == 0:
                    pe.wait_ge(ctx_in[parity], 16 * (turn + 1))
                    pe.wait_ge(x_ready, owed)
                if kind == "keys":
                    if kt == 0:
                        pe.wait_ge(k_copied, MT * c + m + 1)
                    mm = nc.tensor.matmul(pk[:, :], wk[:, kt, P * m:P * (m + 1)], cT[:, parity, kt, :],
                                          start=(kt == 0), stop=(kt == KT - 1))
                    if kt == KT - 1:
                        mm.then_inc(k_ready, 1)
                else:
                    if kt == 0 and jj % 2 == 0:
                        pe.wait_ge(v_copied, JC // 2 * c + m + 1)
                    mm = nc.tensor.matmul(pv[:, jj % 2, :], cT[:, parity, kt, P * jj:P * (jj + 1)], wv[:, kt, :],
                                          start=(kt == 0), stop=(kt == KT - 1))
                    if kt == KT - 1 and jj % 2 == 1:
                        mm.then_inc(v_ready, 1)
                if k == PRODUCTS - 1:
                    pe.wait_ge(v_ready, JC // 2 * (c + 1))
                    pe.sem_inc(ctx_used, 1)

            def scores(unit, local, parity, q0):
                pe.wait_ge(exp_done, unit + 1)
                jt, hp = divmod(local, H // 2)
                for i in range(2):
                    h = 2 * hp + i
                    mm = nc.tensor.matmul(ps[:, local % SRING, i, :], ks[:, parity, h, P * (jt % JC):P * (jt % JC + 1)],
                                          sb["q"][:, h, bass.ds(q0, T)], start=(i == 0), stop=True,
                                          skip_group_check=True)
                mm.then_inc(s_ready, 1)

            def values(group, local):
                par, hg = local // NG % 2, local % NG
                for i in range(GH):
                    h = GH * hg + i
                    mm = nc.tensor.matmul(po[DP * i:DP * (i + 1), hg, :], vs[:, par, h, :], pr[:, par, h, :],
                                          start=False, stop=True, skip_group_check=True)
                mm.then_inc(pv_done, 1)

            pe.sem_inc(pv_done, PRING)
            pe.wait_ge(w_in, 16 * 5)
            for k in range(PRODUCTS):
                project(0, 0, 0, 1, k)
            pe.wait_ge(zeroed, 2)
            pe.wait_ge(k_sent[0], SENT)
            for u in range(2 * AHEAD):
                scores(u, u, 0, 0)
            with pe.Fori(0, B) as b:
                for i in range(GH):
                    for bank in range(2):
                        mm = nc.tensor.matmul(po[DP * i:DP * (i + 1), 2 * bank:2 * bank + 2, :], zero[:, 0:DP],
                                              zero[:, :], start=True, stop=True, skip_group_check=True)
                with pe.Fori(0, NB) as it:
                    n = b * NB + it
                    q0 = b * T
                    for s in range(AHEAD, STEP_GROUPS):
                        cc = s // (STEP_GROUPS // 2)
                        if s == STEP_GROUPS // 2:
                            pe.wait_ge(k_sent[1], SENT * (n + 1))
                        for half in range(2):
                            scores(STEP_UNITS * n + 2 * s + half, 2 * s + half, cc, q0)
                        k = s % (STEP_GROUPS // 2) - AHEAD
                        if 0 <= k < PRODUCTS:
                            if cc == 0:
                                project(2 * n + 1, 1, n, b + 1, k)
                            else:
                                with pe.If(n < NCH // 2 - 1):
                                    project(2 * n + 2, 0, n + 1, b + 1, k)
                        g = s - NG - 2
                        if g >= 0:
                            if g % NG == 0:
                                pe.wait_ge(vs_ready, JC + 2 * JC * n + g // NG + 1)
                            values(STEP_GROUPS * n + g, g)
                    with pe.If(n < NCH // 2 - 1):
                        pe.wait_ge(k_sent[0], SENT * (n + 2))
                        for u in range(2 * AHEAD):
                            scores(STEP_UNITS * (n + 1) + u, u, 0, nc.s_assert_le(((n + 1) // NB) * T, (B - 1) * T))
                    for g in range(STEP_GROUPS - NG - 2, STEP_GROUPS):
                        if g % NG == 0:
                            pe.wait_ge(vs_ready, JC + 2 * JC * n + g // NG + 1)
                        values(STEP_GROUPS * n + g, g)
                pe.wait_ge(o_ready, b + 1)
                pe.wait_ge(k_copied, (MT * 2 * NB) * (b + 1) + 1)
                for t in range(TB):
                    for g in range(NG):
                        mm = nc.tensor.matmul(pk[:, D * t:D * (t + 1)], oT[:, g, P * t:P * (t + 1)], wo[:, g, :],
                                              start=(g == 0), stop=(g == NG - 1), skip_group_check=True)
                mm.then_inc(proj_ready, 1)

        @block.vector
        def _(dve):
            def copy_keys(m, tile):
                dve.wait_ge(k_ready, tile + 1)
                nc.vector.tensor_scalar(kf[:, m, :], pk[:, :], bk[:, m:m + 1], None, ALU.add).then_inc(k_copied, 1)
                dve.wait_ge(k_copied, tile + 2)
                nc.vector.tensor_copy(kp[:, m, 0, :], kf[:, m, :]).then_inc(k_part0, 1)

            def second_part(m, tile):
                dve.wait_ge(k_rest0, tile + 1)
                nc.vector.tensor_copy(kp[:, m, 1, :], kr[:, m, :]).then_inc(k_part1, 1)

            def copy_values(parity, pair, j2):
                dve.wait_ge(v_ready, j2 + 1)
                nc.vector.tensor_tensor(v[:, parity, 2 * pair:2 * pair + 2, :], pv[:, :, :],
                                        bv[:, :].unsqueeze(1).to_broadcast([P, 2, D]), ALU.add).then_inc(v_copied, 1)

            def maximum(unit, local):
                dve.wait_ge(s_ready, unit + 1)
                jt, hp = divmod(local, H // 2)
                nc.vector.tensor_reduce(nmax[:, jt % 2, 2 * hp:2 * hp + 2], ps[:, local % SRING, :, :], AX.X, ALU.max,
                                        negate=True).then_inc(max_ready, 1)

            def invert(j, local):
                dve.wait_ge(exp_done, SRING + (H // 2) * (j + 1))
                dve.wait_ge(vs_ready, JC + j - 1)
                nc.vector.reciprocal(inv[:, local % 2, :], total[:, local % 2, :]).then_inc(inv_ready, 1)

            def side_work(k, c, parity, sent):
                if k == 3:
                    dve.wait_ge(k_sent[1 - parity], sent)
                if k in (3, 8):
                    copy_keys(k // 8, MT * c + k // 8)
                if k in (5, 10):
                    second_part(k // 10, MT * c + k // 10)
                if k in (6, 12):
                    copy_values(parity, k // 12, JC // 2 * c + k // 12)

            dve.sem_inc(k_copied, 1)
            dve.sem_inc(v_copied, 1)
            dve.sem_inc(x_ready, 1)
            dve.wait_ge(w_in, 16 * 5)
            for m in range(MT):
                copy_keys(m, m)
                second_part(m, m)
                copy_values(0, m, m)
            for u in range(2 * AHEAD):
                maximum(u, u)
            with dve.Fori(0, B) as b:
                with dve.Fori(0, NB) as it:
                    n = b * NB + it
                    for s in range(AHEAD, STEP_GROUPS):
                        for half in range(2):
                            maximum(STEP_UNITS * n + 2 * s + half, 2 * s + half)
                        if s % NG == 1 and s > NG:
                            invert(2 * JC * n + s // NG - 1, s // NG - 1)
                        k = s % (STEP_GROUPS // 2) - AHEAD
                        if k in (3, 5, 6, 8, 10, 12):
                            if s < STEP_GROUPS // 2:
                                side_work(k, 2 * n + 1, 1, SENT * (n + 1))
                            else:
                                with dve.If(n < NCH // 2 - 1):
                                    side_work(k, 2 * n + 2, 0, SENT * (n + 1))
                    with dve.If(n < NCH // 2 - 1):
                        for u in range(2 * AHEAD):
                            maximum(STEP_UNITS * (n + 1) + u, u)
                    invert(2 * JC * n + 2 * JC - 1, 2 * JC - 1)
                dve.wait_ge(pv_done, PRING + STEP_GROUPS * NB * (b + 1))
                nc.vector.tensor_copy(oT[:, :, :], po[:, :, :]).then_inc(o_ready, 1)
                dve.wait_ge(proj_ready, b + 1)
                xt = sb["x"][:, bass.ds(TB * b, TB), :]
                nc.vector.tensor_tensor(xt, pk[:, :].rearrange("p (t d) -> p t d", d=D), xt, ALU.add)\
                    .then_inc(x_ready, 1)


def self_attention(nc, dram, sb):
    with ExitStack() as ctx:
        def buf(name, shape, dt=F32):
            return ctx.enter_context(nc.sbuf_tensor(name, shape, dt))

        def sem(name):
            return ctx.enter_context(nc.semaphore(name))

        wqkv, wout, ident = sb["wqkv"], sb["wout"], sb["ident"]
        bout = buf("bout", [P, D])
        logit = buf("logit", [P, 2, HS])
        scale = buf("scale", [P, HS])
        xn = buf("sxn", [P, TB, D])
        sq = buf("ssq", [P, TB, D])
        stat = buf("sstat", [P, 5, TB])
        xnT = buf("sxnT", [P, KT, T])
        qk = buf("qk", [P, TB, 2 * INNER])
        sqr = buf("sqr", [P, 2, 512])
        nst = buf("nst", [P, 4, TB, 2 * HS])
        vv = buf("vv", [P, TB, INNER])
        qkT = buf("qkT", [P, 2 * INNER // P, T])
        nmax = buf("snmax", [P, SR, TB])
        total = buf("stotal", [P, 2, TB])
        inv = buf("sinv", [P, 2, TB])
        pr = buf("spr", [P, 2, TB, T])
        pn = buf("spn", [P, 2, TB, T])
        pT = buf("spT", [P, 2, TB, T])
        aT = buf("aT", [P, INNER // P, T])
        bank = ctx.enter_context(nc.psum_tensor("bank", [P, 8, 512], F32))
        TURN, QKV, QT, SC, PT_, OUT = 0, 1, 5, 0, 3, 5
        PROJ = 7

        logit_in, bout_in = sem("logit_in"), sem("bout_in")
        scaled = sem("scaled")
        ln_step = sem("sln_step")
        root = sem("sroot")
        xt_ready, xt_copied = sem("xt_ready"), sem("xt_copied")
        qkv_ready = sem("qkv_ready")
        squared, qk_copied = sem("squared"), sem("qk_copied")
        summed = sem("summed")
        vv_copied = sem("vv_copied")
        normed = sem("normed")
        qt_ready = sem("qt_ready")
        qt_even, qt_odd = sem("qt_even"), sem("qt_odd")
        s_ready, max_ready, exp_done = sem("ss_ready"), sem("smax_ready"), sem("sexp_done")
        pn_ready, t_ready, t_copied = sem("pn_ready"), sem("t_ready"), sem("t_copied")
        normed_p = sem("normed_p")
        pv_done, o_copied = sem("spv_done"), sem("o_copied")
        out_ready, x_ready = sem("sout_ready"), sem("sx_ready")
        NQK = 2 * INNER // 512 * TB
        NV = INNER // 512 * TB
        VSTEPS = LN_STEPS + 7

        block = ctx.enter_context(nc.Block())

        @block.sync
        def _(sp):
            for e in range(E):
                sp.dma_start(sb["fc"][:, e, :, :], dram["fc"][e]).then_inc(sb["fc_in"], 16)
            sp.dma_start(logit[:, 0, :], dram["logit"]).then_inc(logit_in, 16)
            sp.dma_start(bout[:, :], dram["bout"]).then_inc(bout_in, 16)

        @block.scalar
        def _(act):
            with act.Fori(0, B) as b:
                act.wait_ge(ln_step, VSTEPS * b + LN_VAR)
                nc.scalar.activation(stat[:, 2, :], stat[:, 1, :], ACT.Sqrt).then_inc(root, 1)
                act.wait_ge(xt_ready, b + 1)
                nc.scalar.copy(xnT[:, :, :], bank[:, TURN, :].rearrange("p (k t) -> p k t", k=KT)).then_inc(xt_copied, 1)
                for m in range(NQK):
                    c, t = divmod(m, TB)
                    act.wait_ge(qkv_ready, (NQK + NV) * b + m + 1)
                    if m >= 2:
                        act.wait_ge(summed, NQK * b + m - 1)
                    nc.scalar.activation(sqr[:, m % 2, :], bank[:, QKV + m % 4, :], ACT.Square).then_inc(squared, 1)
                    nc.scalar.copy(qk[:, t, 512 * c:512 * (c + 1)], bank[:, QKV + m % 4, :]).then_inc(qk_copied, 1)
                act.wait_ge(ln_step, VSTEPS * b + LN_STEPS + 1)
                nc.scalar.activation(nst[:, 1, :, :], nst[:, 0, :, :], ACT.Sqrt).then_inc(root, 1)
                for w in range(0, NQK, 2):
                    act.wait_ge(qt_ready, NQK * b + w + 1)
                    nc.scalar.copy(qkT[:, 2 * w:2 * w + 2, :],
                                   bank[:, QT + w % 3, :].rearrange("p (a t) -> p a t", a=2)).then_inc(qt_even, 1)
                for s in range(HS + 2):
                    if s < HS:
                        act.wait_ge(max_ready, HS * b + s + 1)
                        if s >= 2:
                            act.wait_ge(pn_ready, HS * b + s - 1)
                        for i in range(TB):
                            last = nc.scalar.activation(pr[:, s % 2, i, :], bank[:, SC + s % SR, T * i:T * (i + 1)],
                                                        ACT.Exp, bias=nmax[:, s % SR, i:i + 1],
                                                        accum_out=total[:, s % 2, i:i + 1])
                        last.then_inc(exp_done, 1)
                    if s >= 2:
                        h = s - 2
                        act.wait_ge(t_ready, HS * b + h + 1)
                        if h >= 2:
                            act.wait_ge(pv_done, HS * b + h - 1)
                        nc.scalar.copy(pT[:, h % 2, :, :],
                                       bank[:, PT_ + h % 2, :].rearrange("p (j i) -> p j i", j=TB)).then_inc(t_copied, 1)

        @block.tensor
        def _(pe):
            pe.wait_ge(sb["attn_in"], 32)
            with pe.Fori(0, B) as b:
                pe.wait_ge(ln_step, VSTEPS * b + LN_STEPS)
                for k in range(KT):
                    for t in range(TB):
                        mm = nc.tensor.transpose(bank[:, TURN, T * k + P * t:T * k + P * (t + 1)],
                                                 xn[:, t, P * k:P * (k + 1)], ident[:, :])
                mm.then_inc(xt_ready, 1)
                pe.wait_ge(xt_copied, b + 1)
                for m in range(NQK + NV):
                    c, t = divmod(m, TB)
                    if 4 <= m < NQK + 4:
                        pe.wait_ge(qk_copied, NQK * b + m - 3)
                    for k in range(KT):
                        mm = nc.tensor.matmul(bank[:, QKV + m % 4, :], xnT[:, k, P * t:P * (t + 1)],
                                              wqkv[:, k, 512 * c:512 * (c + 1)], start=(k == 0), stop=(k == KT - 1))
                    mm.then_inc(qkv_ready, 1)
                for w in range(NQK):
                    pe.wait_ge(normed, NQK * b + min(NQK, 2 * (w // 2) + 2))
                    if w >= 3:
                        if w % 2:
                            pe.wait_ge(qt_even, NQK // 2 * b + (w - 3) // 2 + 1)
                        else:
                            pe.wait_ge(qt_odd, NQK // 2 * b + (w - 3) // 2 + 1)
                    for a in range(2):
                        for t in range(TB):
                            mm = nc.tensor.transpose(bank[:, QT + w % 3, T * a + P * t:T * a + P * (t + 1)],
                                                     qk[:, t, P * (2 * w + a):P * (2 * w + a + 1)], ident[:, :])
                    mm.then_inc(qt_ready, 1)
                pe.wait_ge(qt_even, NQK // 2 * (b + 1))
                pe.wait_ge(qt_odd, NQK // 2 * (b + 1))
                pe.wait_ge(vv_copied, NV * (b + 1))
                for s in range(HS + 3):
                    if s < HS:
                        if s >= SR:
                            pe.wait_ge(exp_done, HS * b + s - SR + 1)
                        r = slice(DH * (s % 2), DH * (s % 2 + 1))
                        for i in range(TB):
                            mm = nc.tensor.matmul(bank[:, SC + s % SR, T * i:T * (i + 1)],
                                                  qkT[r, s // 2, P * i:P * (i + 1)], qkT[r, HS // 2 + s // 2, :],
                                                  start=True, stop=True, skip_group_check=True)
                        mm.then_inc(s_ready, 1)
                    if 2 <= s < HS + 2:
                        h = s - 2
                        pe.wait_ge(pn_ready, HS * b + h + 1)
                        if h >= 2:
                            pe.wait_ge(t_copied, HS * b + h - 1)
                        for j in range(TB):
                            for i in range(TB):
                                mm = nc.tensor.transpose(bank[:, PT_ + h % 2, T * j + P * i:T * j + P * (i + 1)],
                                                         pn[:, h % 2, i, P * j:P * (j + 1)], ident[:, :])
                        mm.then_inc(t_ready, 1)
                    if s >= 3:
                        h = s - 3
                        pe.wait_ge(t_copied, HS * b + h + 1)
                        if h % 2 == 0 and h >= 4:
                            pe.wait_ge(o_copied, HS // 2 * b + h // 2 - 1)
                        for j in range(TB):
                            mm = nc.tensor.matmul(bank[DH * (h % 2):DH * (h % 2 + 1), OUT + h // 2 % 2, 0:T],
                                                  vv[:, j, DH * h:DH * (h + 1)], pT[:, h % 2, j, :],
                                                  start=(j == 0), stop=(j == TB - 1), skip_group_check=True)
                        mm.then_inc(pv_done, 1)
                pe.wait_ge(o_copied, HS // 2 * (b + 1))
                for t in range(TB):
                    for k in range(INNER // P):
                        mm = nc.tensor.matmul(bank[:, PROJ, D * t:D * (t + 1)], aT[:, k, P * t:P * (t + 1)],
                                              wout[:, k, :], start=(k == 0), stop=(k == INNER // P - 1),
                                              skip_group_check=True)
                mm.then_inc(out_ready, 1)

        @block.vector
        def _(dve):
            dve.wait_ge(logit_in, 16)
            k = 0
            y, t = logit[:, 1, :], scale[:, :]
            steps = [lambda: nc.vector.tensor_scalar(y, logit[:, 0, :], MAX_LOG_SCALE, 1.0 / 64, ALU.min, ALU.mult),
                     lambda: nc.vector.tensor_scalar(t, y, 1.0 / 7, 1.0, ALU.mult, ALU.add)]
            for n in range(6, 0, -1):
                steps.append(lambda: nc.vector.tensor_tensor(t, t, y, ALU.mult))
                steps.append(lambda n=n: nc.vector.tensor_scalar(t, t, 1.0 / n, 1.0, ALU.mult, ALU.add))
            steps += [lambda: nc.vector.tensor_tensor(t, t, t, ALU.mult)] * 6
            for step in steps:
                k += 1
                step().then_inc(scaled, 1)
                dve.wait_ge(scaled, k)
            dve.wait_ge(bout_in, 16)

            with dve.Fori(0, B) as b:
                x = sb["x"][:, bass.ds(TB * b, TB), :]
                base = VSTEPS * b
                layer_norm_vector(dve, nc, x, xn[:, :, :], sq[:, :, :], stat, TB, ln_step, (root, 2 * b + 1), base)
                for m in range(NQK):
                    c, t = divmod(m, TB)
                    dve.wait_ge(squared, NQK * b + m + 1)
                    nc.vector.tensor_reduce(nst[:, 0, t, 8 * c:8 * (c + 1)],
                                            sqr[:, m % 2, :].rearrange("p (h d) -> p h d", d=DH),
                                            AX.X, ALU.add).then_inc(summed, 1)
                for m in range(NV):
                    c, t = divmod(m, TB)
                    dve.wait_ge(qkv_ready, (NQK + NV) * b + NQK + m + 1)
                    nc.vector.tensor_copy(vv[:, t, 512 * c:512 * (c + 1)], bank[:, QKV + (NQK + m) % 4, :])\
                        .then_inc(vv_copied, 1)
                ss, nrm, inn, cor = (nst[:, i, :, :] for i in range(4))
                dve.wait_ge(summed, NQK * (b + 1))
                nc.vector.tensor_scalar(ss, ss, NORM_EPS ** 2, None, ALU.max).then_inc(ln_step, 1)
                base = base + LN_STEPS + 1
                dve.wait_ge(root, 2 * b + 2)
                nc.vector.reciprocal(inn, nrm).then_inc(ln_step, 1)
                dve.wait_ge(ln_step, base + 1)
                nc.vector.tensor_tensor(cor, ss, inn, ALU.mult).then_inc(ln_step, 1)
                dve.wait_ge(ln_step, base + 2)
                nc.vector.tensor_tensor(cor, cor, inn, ALU.mult).then_inc(ln_step, 1)
                dve.wait_ge(ln_step, base + 3)
                nc.vector.tensor_scalar(cor, cor, -0.5, 1.5, ALU.mult, ALU.add).then_inc(ln_step, 1)
                dve.wait_ge(ln_step, base + 4)
                nc.vector.tensor_tensor(inn, inn, cor, ALU.mult).then_inc(ln_step, 1)
                dve.wait_ge(ln_step, base + 5)
                nc.vector.tensor_tensor(inn[:, :, 0:HS], inn[:, :, 0:HS],
                                        scale[:, :].unsqueeze(1).to_broadcast([P, TB, HS]), ALU.mult).then_inc(ln_step, 1)
                dve.wait_ge(ln_step, base + 6)
                dve.wait_ge(qk_copied, NQK * (b + 1))
                for m in range(NQK):
                    c, t = divmod(m, TB)
                    a = qk[:, t, 512 * c:512 * (c + 1)].rearrange("p (h d) -> p h d", d=DH)
                    nc.vector.tensor_tensor(a, a, inn[:, t, 8 * c:8 * (c + 1)].unsqueeze(2).to_broadcast([P, 8, DH]),
                                            ALU.mult).then_inc(normed, 1)
                for w in range(1, NQK, 2):
                    dve.wait_ge(qt_ready, NQK * b + w + 1)
                    nc.vector.tensor_copy(qkT[:, 2 * w:2 * w + 2, :],
                                          bank[:, QT + w % 3, :].rearrange("p (a t) -> p a t", a=2)).then_inc(qt_odd, 1)
                for s in range(HS + 4):
                    if s < HS:
                        dve.wait_ge(s_ready, HS * b + s + 1)
                        nc.vector.tensor_reduce(nmax[:, s % SR, :],
                                                bank[:, SC + s % SR, :].rearrange("p (i j) -> p i j", i=TB),
                                                AX.X, ALU.max, negate=True).then_inc(max_ready, 1)
                    if 1 <= s < HS + 1:
                        h = s - 1
                        dve.wait_ge(exp_done, HS * b + h + 1)
                        if h >= 2:
                            dve.wait_ge(t_ready, HS * b + h - 1)
                        nc.vector.reciprocal(inv[:, h % 2, :], total[:, h % 2, :]).then_inc(normed_p, 1)
                        dve.wait_ge(normed_p, HS * b + h + 1)
                        for i in range(TB):
                            last = nc.vector.tensor_scalar(pn[:, h % 2, i, :], pr[:, h % 2, i, :],
                                                           inv[:, h % 2, i:i + 1], None, ALU.mult)
                        last.then_inc(pn_ready, 1)
                    if s >= 4 and s % 2 == 0 or s == HS + 3:
                        g = (s - 4) // 2 if s % 2 == 0 else HS // 2 - 1
                        if s % 2 == 0 and g < HS // 2 - 1 or s == HS + 3:
                            dve.wait_ge(pv_done, HS * b + 2 * g + 2)
                            nc.vector.tensor_copy(aT[:, g, :], bank[:, OUT + g % 2, 0:T]).then_inc(o_copied, 1)
                dve.wait_ge(out_ready, b + 1)
                nc.vector.tensor_tensor(x, bank[:, PROJ, :].rearrange("p (t d) -> p t d", d=D), x, ALU.add)\
                    .then_inc(x_ready, 1)
                dve.wait_ge(x_ready, 2 * b + 1)
                nc.vector.tensor_tensor(x, x, bout[:, :].unsqueeze(1).to_broadcast([P, TB, D]), ALU.add)\
                    .then_inc(x_ready, 1)


def experts(nc, dram, sb):
    with ExitStack() as ctx:
        def buf(name, shape, dt=F32):
            return ctx.enter_context(nc.sbuf_tensor(name, shape, dt))

        def sem(name):
            return ctx.enter_context(nc.semaphore(name))

        HT = HD // P
        ident, fc = sb["ident"], sb["fc"]
        old = sb["wqkv"][:, :, :].rearrange("p k n -> p (k n)")
        xn = old[:, 0:TT * D].rearrange("p (t d) -> p t d", d=D)
        sq = old[:, TT * D:2 * TT * D].rearrange("p (t d) -> p t d", d=D)
        xnT = old[:, 2 * TT * D:3 * TT * D].rearrange("p (k t) -> p k t", k=KT)
        yg = sb["wout"]
        pj = buf("pj", [P, E, HT, D])
        stat = buf("estat", [P, 5, TT])
        router = buf("router", [P, KT, E])
        before = buf("before", [P, P])
        ones = buf("ones", [P, P])
        rows = buf("rows", [P, 3, 16])
        upto = buf("upto", [P, E, E])
        lg = buf("lg", [P, TT, E])
        best = buf("best", [P, TT])
        mask = buf("mask", [P, TT, E])
        prior = buf("prior", [P, TT + 1, E])
        cube = buf("cube", [P, E, E])
        tiles = buf("tiles", [P, 3, E])
        pos = buf("pos", [P, TT])
        pos_int = buf("pos_int", [P, TT], mybir.dt.uint32)
        past = buf("past", [P, SLOT_TILES, E])
        expert = buf("expert", [P, SLOT_TILES])
        expert_int = buf("expert_int", [P, SLOT_TILES], mybir.dt.int32)
        xs = buf("xs", [P, 3, D])
        xsT = buf("xsT", [P, 3, KT, P])
        rl = buf("rl", [P, HD])
        hs = buf("hs", [P, HD])
        hT = buf("hT", [P, HT, P])
        y = buf("y", [P, 3, D])
        bank = ctx.enter_context(nc.psum_tensor("ebank", [P, 8, 512], F32))
        HID, HTB, XTB, YB = 0, 2, 4, 5

        const_in, router_in = sem("const_in"), sem("router_in")
        pj_in = sem("pj_in")
        ln_step, root = sem("eln_step"), sem("eroot")
        turned, turned_out = sem("eturned"), sem("eturned_out")
        lg_ready = sem("lg_ready")
        step = sem("sort_step")
        cum_ready = sem("cum_ready")
        put = sem("put")
        xs_in = [sem(f"xs_in{i}") for i in range(3)]
        xt_ready, xt_copied = sem("ext_ready"), sem("ext_copied")
        h_ready, h_relu, h_square = sem("h_ready"), sem("h_relu"), sem("h_square")
        ht_ready, ht_low = sem("ht_ready"), sem("ht_low")
        ht_high = sem("ht_high")
        y_ready, y_copied = sem("y_ready"), sem("y_copied")
        y_out = [sem(f"y_out{i}") for i in range(3)]
        got = sem("got")
        SORTED, PRIOR = 29, 15
        LAST = SLOT_TILES - 1

        block = ctx.enter_context(nc.Block())

        def tiles_loop(eng, do):
            do(0, 0, True, False)
            with eng.Fori(0, (SLOT_TILES - 1) // 3) as n:
                for i in range(1, 4):
                    do(3 * n + i, i % 3, False, False)
            for t in range(3 * ((SLOT_TILES - 1) // 3) + 1, SLOT_TILES + 1):
                do(t, t % 3, False, t == SLOT_TILES)

        @block.sync
        def _(sp):
            sp.dma_start(before[:, :], dram["before"]).then_inc(const_in, 16)
            sp.dma_start(ones[:, :], dram["ones"]).then_inc(const_in, 16)
            sp.dma_start(rows[:, :, :], dram["rows"]).then_inc(const_in, 16)
            sp.dma_start(upto[:, :, :], dram["upto"]).then_inc(const_in, 16)
            sp.dma_start(router[:, :, :], dram["router"]).then_inc(router_in, 16)
            for e in range(E):
                sp.dma_start(pj[:, e, :, :], dram["pj"][e]).then_inc(pj_in, 16)
            sp.wait_ge(put, 16 * TT)

            def load(t, slot):
                sp.dma_start(xs[:, slot, :], dram["sorted_x"][bass.ds(t, 1), :, :]).then_inc(xs_in[slot], 16)

            for i in range(3):
                load(i, i)

            def store(t, slot):
                sp.wait_ge(y_copied, t + 2)
                sp.dma_start(dram["sorted_y"][bass.ds(t, 1), :, :], y[:, slot, :]).then_inc(y_out[slot], 16)

            for i in range(3):
                sp.sem_inc(y_out[i], 16)
            with sp.Fori(0, SLOT_TILES // 3 - 1) as n:
                for i in range(3):
                    sp.wait_ge(xt_ready, 3 * n + i + 1)
                    load(3 * n + i + 3, i)
                    store(3 * n + i, i)
            for t in range(SLOT_TILES - 3, SLOT_TILES):
                store(t, t % 3)

        @block.gpsimd
        def _(pool):
            pool.wait_ge(step, SORTED)
            for t in range(TT):
                nc.gpsimd.indirect_dma_start(dram["sorted_x"].rearrange("a p d -> (a p) d"),
                                             bass.IndirectOffsetOnAxis(ap=pos_int[:, t:t + 1], axis=0),
                                             xn[:, t, :], None).then_inc(put, 16)
            for i in range(3):
                pool.wait_ge(y_out[i], 16 * (SLOT_TILES // 3 + 1))
            for t in range(TT):
                nc.gpsimd.indirect_dma_start(yg[:, t, :], None, dram["sorted_y"].rearrange("a p d -> (a p) d"),
                                             bass.IndirectOffsetOnAxis(ap=pos_int[:, t:t + 1], axis=0))\
                    .then_inc(got, 16)

        @block.scalar
        def _(act):
            act.wait_ge(ln_step, LN_VAR)
            nc.scalar.activation(stat[:, 2, :], stat[:, 1, :], ACT.Sqrt).then_inc(root, 1)
            for b in range(4):
                act.wait_ge(turned, b + 1)
                half, k = b % 2, b // 2
                nc.scalar.copy(xnT[:, k, 512 * half:512 * (half + 1)], bank[:, b, :]).then_inc(turned_out, 1)

            def do(t, slot, first, last):
                static = isinstance(t, int)
                if not static or t + 1 <= LAST:
                    act.wait_ge(xt_ready, t + 2)
                    nc.scalar.copy(xsT[:, (slot + 1) % 3, :, :],
                                   bank[:, XTB, 0:D].rearrange("p (k t) -> p k t", k=KT)).then_inc(xt_copied, 1)
                if not first:
                    act.wait_ge(ht_ready, t)
                    nc.scalar.copy(hT[:, 0:HT // 2, :], bank[:, HTB, :].rearrange("p (a t) -> p a t", t=P))\
                        .then_inc(ht_low, 1)
                if not last:
                    act.wait_ge(h_ready, t + 1)
                    nc.scalar.activation(rl[:, :], bank[:, HID:HID + 2, :].rearrange("p a n -> p (a n)"), ACT.Relu)\
                        .then_inc(h_relu, 1)

            act.wait_ge(xt_ready, 1)
            nc.scalar.copy(xsT[:, 0, :, :], bank[:, XTB, 0:D].rearrange("p (k t) -> p k t", k=KT)).then_inc(xt_copied, 1)
            tiles_loop(act, do)

        @block.tensor
        def _(pe):
            pe.wait_ge(ln_step, LN_STEPS)
            for b in range(4):
                half, k = b % 2, b // 2
                for i in range(4):
                    last = nc.tensor.transpose(bank[:, b, P * i:P * (i + 1)],
                                               xn[:, 4 * half + i, P * k:P * (k + 1)], ident[:, :])
                last.then_inc(turned, 1)
            pe.wait_ge(router_in, 16)
            pe.wait_ge(turned_out, 4)
            for t in range(TT):
                for k in range(KT):
                    mm = nc.tensor.matmul(bank[:, 7, E * t:E * (t + 1)], xnT[:, k, P * t:P * (t + 1)], router[:, k, :],
                                          start=(k == 0), stop=(k == KT - 1), skip_group_check=True)
            mm.then_inc(lg_ready, 1)
            pe.wait_ge(const_in, 64)
            pe.wait_ge(step, PRIOR)
            nc.tensor.matmul(bank[:, 6, 0:(TT + 1) * E], ones[:, :], prior[:, :, :].rearrange("p t e -> p (t e)"),
                             start=True, stop=True, skip_group_check=True)
            nc.tensor.matmul(bank[:, 6, 0:TT * E], before[:, :], mask[:, :, :].rearrange("p t e -> p (t e)"),
                             start=False, stop=True, skip_group_check=True).then_inc(cum_ready, 1)

            def turn_rows(t, slot):
                pe.wait_ge(xs_in[slot], 16 * (t // 3 + 1) if isinstance(t, int) else 16 * turn_of(t, slot))
                pe.wait_ge(xt_copied, t)
                for k in range(KT):
                    mm = nc.tensor.transpose(bank[:, XTB, P * k:P * (k + 1)], xs[:, slot, P * k:P * (k + 1)], ident[:, :])
                mm.then_inc(xt_ready, 1)

            def turn_of(t, slot):
                return (t - slot) // 3 + 1

            def do(t, slot, first, last):
                if not first:
                    pe.wait_ge(h_square, t)
                    pe.wait_ge(ht_high, t)
                    for a in range(HT):
                        mm = nc.tensor.transpose(bank[:, HTB + a // 4, P * (a % 4):P * (a % 4 + 1)],
                                                 hs[:, P * a:P * (a + 1)], ident[:, :])
                    mm.then_inc(ht_ready, 1)
                if not isinstance(t, int) or t + 1 <= LAST:
                    turn_rows(t + 1, (slot + 1) % 3)
                if not last:
                    e = pe.value_load(expert_int[0:1, bass.ds(t, 1)], min_val=0, max_val=E - 1)
                    pe.wait_ge(xt_copied, t + 1)
                    for c in range(2):
                        for k in range(KT):
                            mm = nc.tensor.matmul(bank[:, HID + c, :], xsT[:, slot, k, :],
                                                  fc[:, bass.ds(e, 1), k, 512 * c:512 * (c + 1)],
                                                  start=(k == 0), stop=(k == KT - 1))
                    mm.then_inc(h_ready, 1)
                if first:
                    pe.wait_ge(pj_in, 16 * E)
                else:
                    e = pe.value_load(expert_int[0:1, bass.ds(t - 1, 1)], min_val=0, max_val=E - 1)
                    pe.wait_ge(ht_low, t)
                    pe.wait_ge(ht_high, t + 1)
                    pe.wait_ge(y_copied, t)
                    for a in range(HT):
                        mm = nc.tensor.matmul(bank[:, YB, 0:D], hT[:, a, :], pj[:, bass.ds(e, 1), a, :],
                                              start=(a == 0), stop=(a == HT - 1))
                    mm.then_inc(y_ready, 1)

            pe.wait_ge(step, SORTED)
            pe.wait_ge(sb["fc_in"], 16 * E)
            turn_rows(0, 0)
            tiles_loop(pe, do)

        @block.vector
        def _(dve):
            layer_norm_vector(dve, nc, sb["x"][:, :, :], xn, sq, stat, TT, ln_step, (root, 1), 0)
            dve.wait_ge(lg_ready, 1)
            dve.wait_ge(const_in, 64)
            k = [0]

            def link(ins):
                k[0] += 1
                ins.then_inc(step, 1)
                dve.wait_ge(step, k[0])

            def across(a, shape):
                return a.unsqueeze(1).to_broadcast(shape)

            def along(a, shape):
                return a.unsqueeze(2).to_broadcast(shape)

            te, ee, se = [P, TT, E], [P, E, E], [P, SLOT_TILES, E]
            link(nc.vector.tensor_copy(lg[:, :, :], bank[:, 7, 0:TT * E].rearrange("p (t e) -> p t e", e=E)))
            link(nc.vector.tensor_reduce(best[:, :], lg[:, :, :], AX.X, ALU.max))
            link(nc.vector.tensor_tensor(lg[:, :, :], lg[:, :, :], along(best[:, :], te), ALU.is_equal))
            link(nc.vector.tensor_tensor(lg[:, :, :], lg[:, :, :], across(rows[:, 0, 0:E], te), ALU.mult))
            link(nc.vector.tensor_reduce(best[:, :], lg[:, :, :], AX.X, ALU.max))
            link(nc.vector.tensor_tensor(mask[:, :, :], lg[:, :, :], along(best[:, :], te), ALU.is_equal))
            link(nc.vector.memset(prior[:, 0, :], 0.0))
            for t in range(TT):
                link(nc.vector.tensor_tensor(prior[:, t + 1, :], prior[:, t, :], mask[:, t, :], ALU.add))
            assert k[0] == PRIOR
            dve.wait_ge(cum_ready, 1)
            link(nc.vector.tensor_copy(tiles[:, 0, :], bank[:, 6, TT * E:(TT + 1) * E]))
            link(nc.vector.tensor_tensor(cube[:, :, :], along(tiles[:, 0, :], ee), across(rows[:, 1, 0:E], ee), ALU.is_gt))
            link(nc.vector.tensor_reduce(tiles[:, 0, :], cube[:, :, :], AX.X, ALU.add))
            link(nc.vector.tensor_tensor(cube[:, :, :], across(tiles[:, 0, :], ee), upto[:, :, :], ALU.mult))
            link(nc.vector.tensor_reduce(tiles[:, 1, :], cube[:, :, :], AX.X, ALU.add))
            link(nc.vector.tensor_tensor(tiles[:, 2, :], tiles[:, 1, :], tiles[:, 0, :], ALU.subtract))
            link(nc.vector.tensor_tensor(past[:, :, :], across(tiles[:, 1, :], se),
                                         along(rows[:, 2, 0:SLOT_TILES], se), ALU.is_le))
            link(nc.vector.tensor_reduce(expert[:, :], past[:, :, :], AX.X, ALU.add))
            link(nc.vector.tensor_scalar(expert_int[:, :], expert[:, :], float(E - 1), None, ALU.min))
            link(nc.vector.tensor_scalar(tiles[:, 2, :], tiles[:, 2, :], float(P), None, ALU.mult))
            link(nc.vector.tensor_tensor(lg[:, :, :], bank[:, 6, 0:TT * E].rearrange("p (t e) -> p t e", e=E),
                                         across(tiles[:, 2, :], te), ALU.add))
            link(nc.vector.tensor_tensor(lg[:, :, :], lg[:, :, :], mask[:, :, :], ALU.mult))
            link(nc.vector.tensor_reduce(pos[:, :], lg[:, :, :], AX.X, ALU.add))
            assert k[0] == SORTED - 1
            nc.vector.tensor_copy(pos_int[:, :], pos[:, :]).then_inc(step, 1)

            def do(t, slot, first, last):
                if not first:
                    dve.wait_ge(ht_ready, t)
                    nc.vector.tensor_copy(hT[:, HT // 2:HT, :], bank[:, HTB + 1, :].rearrange("p (a t) -> p a t", t=P))\
                        .then_inc(ht_high, 1)
                if not last:
                    dve.wait_ge(h_relu, t + 1)
                    nc.vector.tensor_tensor(hs[:, :], rl[:, :], rl[:, :], ALU.mult).then_inc(h_square, 1)
                if not first:
                    dve.wait_ge(y_ready, t)
                    dve.wait_ge(y_out[(slot + 2) % 3], 16 * ((t - 1 - (slot + 2) % 3) // 3 + 1))
                    nc.vector.tensor_copy(y[:, (slot + 2) % 3, :], bank[:, YB, 0:D]).then_inc(y_copied, 1)

            dve.sem_inc(ht_high, 1)
            dve.sem_inc(y_copied, 1)
            tiles_loop(dve, do)
            dve.wait_ge(got, 16 * TT)
            nc.vector.tensor_tensor(sb["x"][:, :, :], sb["x"][:, :, :], yg[:, :, :], ALU.add).then_inc(step, 1)


def finish(nc, dram, sb):
    with ExitStack() as ctx:
        out_sent = ctx.enter_context(nc.semaphore("out_sent"))
        block = ctx.enter_context(nc.Block())

        @block.sync
        def _(sp):
            sp.dma_start(dram["out"].rearrange("(t p) d -> p t d", p=P), sb["x"][:, :, :]).then_inc(out_sent, 16)
            sp.wait_ge(out_sent, 16)


def program(nc, dram):
    with ExitStack() as ctx:
        def buf(name, shape, dt=F32):
            return ctx.enter_context(nc.sbuf_tensor(name, shape, dt))

        sb = {
            "x": buf("x", [P, TT, D]),
            "ident": buf("ident", [P, P]),
        }
        sb["fc_in"] = ctx.enter_context(nc.semaphore("fc_in"))
        sb["zeroed_rows"] = ctx.enter_context(nc.semaphore("zeroed_rows"))
        sb["attn_in"] = ctx.enter_context(nc.semaphore("attn_in"))
        with nc.sbuf_tensor("wqkv", [P, KT, 3 * INNER], F32) as sb["wqkv"], \
                nc.sbuf_tensor("wout", [P, INNER // P, D], F32) as sb["wout"]:
            with nc.sbuf_tensor("q_stacked", [KR, H, B * T], BF16) as sb["q"]:
                prepare(nc, dram, sb)
                cross_attention(nc, dram, sb)
            with nc.sbuf_tensor("fc", [P, E, KT, HD], F32) as sb["fc"]:
                self_attention(nc, dram, sb)
                experts(nc, dram, sb)
        finish(nc, dram, sb)


def kernel(x, ctx_1024, L0_xattn_Wq, L0_xattn_bq, L0_xattn_Wk, L0_xattn_bk, L0_xattn_Wv, L0_xattn_bv, L0_xattn_Wo,
           L0_xattn_bo, L0_attn_w_qkv, L0_attn_w_out, L0_attn_b_out, L0_attn_logit_scale, L0_ffn_router_w,
           L0_ffn_expert_fc, L0_ffn_expert_proj):
    import numpy as np
    import concourse.bacc as bacc
    from concourse.bass_utils import run_bass_kernel_spmd

    def rows(w):
        w = np.asarray(w)
        return w.reshape(w.shape[0] // P, P, -1).transpose(1, 0, 2)

    def by_width(w):
        w = np.asarray(w)
        return w.reshape(-1, MT, HM, DK).transpose(0, 1, 3, 2).reshape(-1, D)

    def every(v):
        return np.broadcast_to(np.asarray(v).reshape(1, -1), (P, np.asarray(v).size))

    wo = np.zeros((NG, GH, DP, D), np.float32)
    wo[:, :, :DK, :] = np.asarray(L0_xattn_Wo).reshape(NG, GH, DK, D)
    lane = np.arange(16, dtype=np.float32)
    arrays = {
        "x": np.asarray(x).reshape(B * T, D),
        "ctxT": np.asarray(ctx_1024).reshape(NCH, CH, KT, P).transpose(0, 3, 2, 1),
        "wq": rows(by_width(L0_xattn_Wq)),
        "bq": by_width(np.asarray(L0_xattn_bq)[None]).reshape(MT, P).T,
        "wk": rows(by_width(L0_xattn_Wk)),
        "bk": by_width(np.asarray(L0_xattn_bk)[None]).reshape(MT, P).T,
        "wv": rows(L0_xattn_Wv),
        "bv": every(L0_xattn_bv),
        "wo": wo.reshape(NG, P, D).transpose(1, 0, 2),
        "bo": every(L0_xattn_bo),
        "wqkv": rows(L0_attn_w_qkv),
        "wout": rows(L0_attn_w_out),
        "bout": every(L0_attn_b_out),
        "logit": every(L0_attn_logit_scale),
        "before": np.triu(np.ones((P, P), np.float32), 1),
        "ones": np.ones((P, P), np.float32),
        "rows": np.broadcast_to(np.stack([E - lane, P * lane, lane]), (P, 3, 16)),
        "upto": np.broadcast_to(np.tril(np.ones((E, E), np.float32)), (P, E, E)),
        "router": rows(np.asarray(L0_ffn_router_w).T),
        "fc": np.asarray(L0_ffn_expert_fc).reshape(E, KT, P, HD).transpose(0, 2, 1, 3),
        "pj": np.asarray(L0_ffn_expert_proj).reshape(E, D, HD // P, P).transpose(0, 3, 2, 1),
    }
    nc = bacc.Bacc("TRN2", target_bir_lowering=False, num_devices=1)
    dram = {}
    for name, a in arrays.items():
        arrays[name] = a = np.ascontiguousarray(a)
        dram[name] = nc.dram_tensor(f"{name}_dram", a.shape, mybir.dt.from_np(a.dtype), kind="ExternalInput").ap()
    for name in ("sorted_x", "sorted_y"):
        dram[name] = nc.dram_tensor(name, (SLOT_TILES, P, D), F32, kind="Internal").ap()
    dram["out"] = nc.dram_tensor("out_dram", (B * T, D), F32, kind="ExternalOutput").ap()
    program(nc, dram)
    r = run_bass_kernel_spmd(nc, [{f"{k}_dram": a for k, a in arrays.items()}], core_ids=[0])
    return r.results[0]["out_dram"].reshape(B, T, D)
```

```python
from contextlib import ExitStack

import concourse.bass as bass
from concourse import mybir

F32 = mybir.dt.float32
BF16 = mybir.dt.bfloat16
ALU = mybir.AluOpType
ACT = mybir.ActivationFunctionType
AX = mybir.AxisListType

P = 128
B, T, D = 4, 256, 256
S = 4096
H = 16
DK = D // H
KT = D // P
TT = B * T // P
TB = T // P
EPS = 1e-5

CH = 512
NCH = B * S // CH
NB = S // CH // 2
JC = CH // P
MT = D // P
HM = H // MT
PARTS = 3
PAIRS = [(0, 0), (0, 1), (0, 2), (1, 0), (1, 1), (2, 0)]
KR = DK * len(PAIRS)
GH = 4
NG = H // GH
STEP_GROUPS = 2 * JC * NG
STEP_UNITS = 2 * STEP_GROUPS
SRING = 4
PRING = 2 * NG
PRODUCTS = MT * KT + JC * KT
ORDER = [("keys", 0, 0, k) for k in range(KT)] + [("values", 0, 0, k) for k in range(KT)] \
    + [("keys", 1, 0, k) for k in range(KT)] + [("values", 0, 1, k) for k in range(KT)] \
    + [("values", 1, j, k) for j in (2, 3) for k in range(KT)]
SLOT = {k: k + 2 * (k >= 8) for k in range(PRODUCTS)}
LAG = NG + 3
AHEAD = 2

HS, DH = 16, 64
INNER = HS * DH
SR = 3
TLAG = 3
MAX_LOG_SCALE = 4.605170185988092
NORM_EPS = 1e-12

E, HD = 8, 4 * D
SLOT_TILES = TT + E - 1
DP = 32


def layer_norm_vector(dve, nc, x, out, stat, t0, t1, step, root, part=0):
    var, std, inv, corr = (stat[:, t0:t1, i] for i in range(7, 11))
    base = part * (LN_INV + EARLY)
    k = [0]

    def link(ins):
        k[0] += 1
        ins.then_inc(step, 1)
        dve.wait_ge(step, base + k[0])

    for t in range(t0, t1):
        last = nc.vector.bn_stats(stat[:, t, 0:6], x[:, t, :])
    link(last)
    for t in range(t0, t1):
        last = nc.vector.bn_aggr(stat[:, t, 6:8], stat[:, t, 0:6])
    link(last)
    nc.vector.tensor_scalar(var, var, EPS, None, ALU.add).then_inc(step, 1)
    dve.wait_ge(root, part + 1)
    k[0] += 1
    assert k[0] == LN_VAR
    link(nc.vector.reciprocal(inv, std))
    link(nc.vector.tensor_tensor(corr, var, inv, ALU.mult))
    link(nc.vector.tensor_tensor(corr, corr, inv, ALU.mult))
    link(nc.vector.tensor_scalar(corr, corr, -0.5, 1.5, ALU.mult, ALU.add))
    link(nc.vector.tensor_tensor(inv, inv, corr, ALU.mult))
    assert k[0] == LN_INV
    for t in range(t0, t1):
        nc.vector.tensor_scalar(out[:, t, :], x[:, t, :], stat[:, t, 6:7], stat[:, t, 9:10],
                                ALU.subtract, ALU.mult).then_inc(step, 1)


LN_VAR = 3
LN_INV = 8
EARLY = TT - TB
LN_ALL = 2 * LN_INV + TT


def layer_norm_root(act, nc, stat, t0, t1, step, root, part=0):
    act.wait_ge(step, part * (LN_INV + EARLY) + LN_VAR)
    nc.scalar.activation(stat[:, t0:t1, 8], stat[:, t0:t1, 7], ACT.Sqrt).then_inc(root, 1)


def turn_half(pe, nc, xn, banks, ident, half, turned):
    for k in range(KT):
        for i in range(4):
            last = nc.tensor.transpose(banks[k][:, P * i:P * (i + 1)], xn[:, 4 * half + i, P * k:P * (k + 1)], ident)
        last.then_inc(turned, 1)


def copy_half(act, nc, xnT, banks, half, turned, turned_out):
    for k in range(KT):
        act.wait_ge(turned, KT * half + k + 1)
        nc.scalar.copy(xnT[:, k, 4 * P * half:4 * P * (half + 1)], banks[k]).then_inc(turned_out, 1)


def cross_attention(nc, dram, sb):
    with ExitStack() as ctx:
        def buf(name, shape, dt=F32):
            return ctx.enter_context(nc.sbuf_tensor(name, shape, dt))

        def sem(name):
            return ctx.enter_context(nc.semaphore(name))

        wk = buf("wk", [P, KT, D])
        wv = buf("wv", [P, KT, D])
        bk = buf("bk", [P, MT])
        bv = buf("bv", [P, D])
        wo = buf("wo", [P, NG, D])
        zero = buf("zero", [P, 512], BF16)
        cT = buf("cT", [P, 2, KT, CH])
        kf = buf("kf", [P, MT, CH])
        kr = buf("kr", [P, MT, CH])
        kp = buf("kp", [P, MT, PARTS, CH], BF16)
        ks = buf("ks", [KR, 2, H, CH], BF16)
        v = buf("v", [P, 2, JC, D])
        vs = buf("vs", [P, 2, H, DP])
        nmax = buf("nmax", [P, 2, H])
        total = buf("total", [P, 2, H])
        inv = buf("inv", [P, 2, H])
        pr = buf("pr", [P, 2, H, T])
        oT = buf("oT", [P, NG, T])
        early = pr[:, :, :, :].rearrange("p a h t -> p (a h t)")
        wq = early[:, 0:KT * D].rearrange("p (k d) -> p k d", d=D)
        bo = early[:, KT * D:(KT + 1) * D]
        xnT = early[:, TT * D:2 * TT * D].rearrange("p (k t) -> p k t", k=KT)
        qf = early[:, 2 * TT * D:3 * TT * D].rearrange("p (m t) -> p m t", m=MT)
        qr = early[:, 3 * TT * D:4 * TT * D].rearrange("p (m t) -> p m t", m=MT)
        qp = buf("qp", [P, MT, PARTS, B * T], BF16)
        stat = buf("qstat", [P, TT, 11])
        bq = buf("bq", [P, MT])
        xn = sb["xn"]
        zrow = sb["wout"][:, 0:3, :]
        ps = ctx.enter_context(nc.psum_tensor("ps", [P, SRING, 2, T], F32))
        po = ctx.enter_context(nc.psum_tensor("po", [P, NG, T], F32))
        pk = ctx.enter_context(nc.psum_tensor("pk", [P, CH], F32))
        pv = ctx.enter_context(nc.psum_tensor("pv", [P, 2, D], F32))

        x_in, wq_in, bo_in = sem("x_in"), sem("wq_in"), sem("bo_in")
        wk_in, wv_in, wo_in = sem("wk_in"), sem("wv_in"), sem("wo_in")
        ident_ready = sem("ident_ready")
        zrow_ready = sem("zrow_ready")
        rows_zeroed = sem("rows_zeroed")
        ln_step, ln_root = sem("ln_step"), sem("ln_root")
        turned, turned_out = sem("turned"), sem("turned_out")
        q_ready = sem("q_ready")
        q_step, q_split = sem("q_step"), sem("q_split")
        q_sent = [sem(f"q_sent{m}") for m in range(MT)]
        x_biased = sem("x_biased")
        zeroed = sem("zeroed")
        ctx_in = [sem("ctx_in0"), sem("ctx_in1")]
        ctx_used = sem("ctx_used")
        k_ready = sem("k_ready")
        k_copied = sem("k_copied")
        k_part0 = sem("k_part0")
        k_rest0 = sem("k_rest0")
        k_part1 = sem("k_part1")
        k_parts = sem("k_parts")
        k_sent = [sem("k_sent0"), sem("k_sent1")]
        v_ready = sem("v_ready")
        v_copied = sem("v_copied")
        s_ready = sem("s_ready")
        max_ready = sem("max_ready")
        exp_done = sem("exp_done")
        inv_ready = sem("inv_ready")
        vs_ready = sem("vs_ready")
        pv_done = sem("pv_done")
        o_ready = sem("o_ready")
        proj_ready = sem("proj_ready")
        x_ready = sem("x_ready")
        SENT = 16 * MT * len(PAIRS)

        block = ctx.enter_context(nc.Block())

        @block.sync
        def _(sp):
            def load(c, parity):
                sp.dma_start(cT[:, parity, :, :], dram["ctxT"][bass.ds(c, 1), :, :, :]).then_inc(ctx_in[parity], 16)

            def send(m, tile, parity):
                sp.wait_ge(k_parts, tile + 1)
                for r, (part, _) in enumerate(PAIRS):
                    sp.dma_start(ks[DK * r:DK * (r + 1), parity, HM * m:HM * (m + 1), :], kp[:, m, part, :])\
                        .then_inc(k_sent[parity], 16)

            sp.dma_start(sb["x"][:, :, :], dram["x"].rearrange("(t p) d -> p t d", p=P)).then_inc(x_in, 16)
            load(0, 0)
            sp.dma_start(wk[:, :, :], dram["wk"]).then_inc(wk_in, 16)
            sp.dma_start(bk[:, :], dram["bk"]).then_inc(wk_in, 16)
            sp.dma_start(wv[:, :, :], dram["wv"]).then_inc(wv_in, 16)
            sp.dma_start(bv[:, :], dram["bv"]).then_inc(wv_in, 16)
            sp.dma_start(wq[:, :, :], dram["wq"]).then_inc(wq_in, 16)
            sp.dma_start(bq[:, :], dram["bq"]).then_inc(wq_in, 16)
            sp.dma_start(bo, dram["bo"]).then_inc(bo_in, 16)
            load(1, 1)
            sp.dma_start(wo[:, :, :], dram["wo"]).then_inc(wo_in, 16)
            for m in range(MT):
                send(m, m, 0)
                sp.wait_ge(q_split, m + 1)
                for r, (_, part) in enumerate(PAIRS):
                    sp.dma_start(sb["q"][DK * r:DK * (r + 1), HM * m:HM * (m + 1), :], qp[:, m, part, :])\
                        .then_inc(q_sent[m], 16)
            sp.dma_start(sb["wqkv"][:, :, :], dram["wqkv"]).then_inc(sb["attn_in"], 16)
            sp.wait_ge(zrow_ready, 1)
            for t in range(0, SLOT_TILES, 3):
                sp.dma_start(dram["sorted_x"][t:t + 3].rearrange("t p d -> p t d"), zrow[:, :, :])\
                    .then_inc(rows_zeroed, 16)
            with sp.Fori(0, NCH // 2) as n:
                with sp.If(n < NCH // 2 - 1):
                    sp.wait_ge(ctx_used, 2 * n + 1)
                    load(nc.s_assert_le(2 * n + 2, NCH - 1), 0)
                sp.wait_ge(s_ready, STEP_UNITS * n + 1)
                for m in range(MT):
                    send(m, MT * (2 * n + 1) + m, 1)
                with sp.If(n < NCH // 2 - 1):
                    sp.wait_ge(ctx_used, 2 * n + 2)
                    load(nc.s_assert_le(2 * n + 3, NCH - 1), 1)
                    sp.wait_ge(s_ready, STEP_UNITS * n + STEP_UNITS // 2)
                    for m in range(MT):
                        send(m, MT * (2 * n + 2) + m, 0)
            sp.wait_ge(rows_zeroed, 16 * (SLOT_TILES // 3))
            sp.dma_start(sb["wout"][:, :, :], dram["wout"]).then_inc(sb["attn_in"], 16)

        @block.gpsimd
        def _(pool):
            nc.gpsimd.memset(sb["ident"][:, :], 0.0).then_inc(ident_ready, 1)
            pool.wait_ge(ident_ready, 1)
            nc.gpsimd.affine_select(out=sb["ident"][:, :], in_=sb["ident"][:, :], compare_op=ALU.not_equal,
                                    fill=1.0, base=0, pattern=[[-1, P]], channel_multiplier=1)\
                .then_inc(ident_ready, 1)
            nc.gpsimd.memset(vs[:, :, :, :], 0.0).then_inc(zeroed, 1)
            nc.gpsimd.memset(zero[:, :], 0.0).then_inc(zeroed, 1)
            pool.wait_ge(zeroed, 2)
            pool.sem_inc(vs_ready, JC)
            nc.gpsimd.memset(zrow[:, :, :], 0.0).then_inc(zrow_ready, 1)
            def rest0(m, tile):
                pool.wait_ge(k_part0, tile + 1)
                nc.gpsimd.tensor_tensor(kr[:, m, :], kf[:, m, :], kp[:, m, 0, :], ALU.subtract).then_inc(k_rest0, 1)

            def rest1(m, tile):
                pool.wait_ge(k_part1, tile + 1)
                nc.gpsimd.tensor_tensor(kp[:, m, 2, :], kr[:, m, :], kp[:, m, 1, :], ALU.subtract).then_inc(k_parts, 1)

            def scale_values(j, parity, slot):
                pool.wait_ge(inv_ready, j + 1)
                pool.wait_ge(pv_done, PRING + NG * (j - 1))
                nc.gpsimd.tensor_tensor(
                    vs[:, slot % 2, :, 0:DK], v[:, parity, slot % JC, :].rearrange("p (h d) -> p h d", d=DK),
                    inv[:, slot % 2, :].unsqueeze(2).to_broadcast([P, H, DK]), ALU.mult).then_inc(vs_ready, 1)

            for m in range(MT):
                rest0(m, m)
                rest1(m, m)
            pool.wait_ge(bo_in, 16)
            pool.wait_ge(ln_step, LN_INV + TT)
            nc.gpsimd.tensor_tensor(sb["x"][:, :, :], sb["x"][:, :, :],
                                    bo.unsqueeze(1).to_broadcast([P, TT, D]), ALU.add).then_inc(x_biased, 1)
            with pool.Fori(0, NCH // 2) as n:
                for slot in range(2 * JC):
                    cc, jj = divmod(slot, JC)
                    if jj < MT and cc == 0:
                        rest0(jj, MT * (2 * n + 1) + jj)
                    if jj < MT and cc == 1:
                        with pool.If(n < NCH // 2 - 1):
                            rest0(jj, MT * (2 * n + 2) + jj)
                    scale_values(2 * JC * n + slot, cc, slot)
                    if jj < MT and cc == 0:
                        rest1(jj, MT * (2 * n + 1) + jj)
                    if jj < MT and cc == 1:
                        with pool.If(n < NCH // 2 - 1):
                            rest1(jj, MT * (2 * n + 2) + jj)

        @block.scalar
        def _(act):
            banks = ps[:, :, :, :].rearrange("p b i t -> p b (i t)")
            layer_norm_root(act, nc, stat, 0, TT, ln_step, ln_root)
            for half in range(2):
                copy_half(act, nc, xnT, [banks[:, KT * half + k, :] for k in range(KT)], half, turned, turned_out)
            act.sem_inc(exp_done, SRING)
            with act.Fori(0, B) as b:
                for g in range(NB * STEP_GROUPS):
                    act.wait_ge(pv_done, NB * STEP_GROUPS * b + g + 1)
                    par, hg = g // NG % 2, g % NG
                    for half in range(2):
                        act.wait_ge(max_ready, NB * STEP_UNITS * b + 2 * g + half + 1)
                        for i in range(2):
                            h = GH * hg + 2 * half + i
                            last = nc.scalar.activation(pr[:, par, h, :], ps[:, (2 * g + half) % SRING, i, :], ACT.Exp,
                                                        bias=nmax[:, par, h:h + 1], accum_out=total[:, par, h:h + 1])
                        last.then_inc(exp_done, 1)
            layer_norm_root(act, nc, sb["stat"], 0, EARLY, sb["ln2_step"], sb["ln2_root"])

        @block.tensor
        def _(pe):
            def project(c, parity, turn, owed, k):
                kind, m, jj, kt = ORDER[k]
                if k == 0:
                    pe.wait_ge(ctx_in[parity], 16 * (turn + 1))
                    pe.wait_ge(x_ready, owed)
                if kind == "keys":
                    if kt == 0:
                        pe.wait_ge(k_copied, MT * c + m + 1)
                    mm = nc.tensor.matmul(pk[:, :], wk[:, kt, P * m:P * (m + 1)], cT[:, parity, kt, :],
                                          start=(kt == 0), stop=(kt == KT - 1))
                    if kt == KT - 1:
                        mm.then_inc(k_ready, 1)
                else:
                    if kt == 0 and jj % 2 == 0:
                        pe.wait_ge(v_copied, JC // 2 * c + m + 1)
                    mm = nc.tensor.matmul(pv[:, jj % 2, :], cT[:, parity, kt, P * jj:P * (jj + 1)], wv[:, kt, :],
                                          start=(kt == 0), stop=(kt == KT - 1))
                    if kt == KT - 1 and jj % 2 == 1:
                        mm.then_inc(v_ready, 1)
                if k == PRODUCTS - 1:
                    pe.wait_ge(v_ready, JC // 2 * (c + 1))
                    pe.sem_inc(ctx_used, 1)

            def scores(unit, local, parity, q0):
                pe.wait_ge(exp_done, unit + 1)
                jt, hp = divmod(local, H // 2)
                for i in range(2):
                    h = 2 * hp + i
                    mm = nc.tensor.matmul(ps[:, local % SRING, i, :], ks[:, parity, h, P * (jt % JC):P * (jt % JC + 1)],
                                          sb["q"][:, h, bass.ds(q0, T)], start=(i == 0), stop=True,
                                          skip_group_check=True)
                mm.then_inc(s_ready, 1)

            def values(group, local):
                par, hg = local // NG % 2, local % NG
                for i in range(GH):
                    h = GH * hg + i
                    mm = nc.tensor.matmul(po[DP * i:DP * (i + 1), hg, :], vs[:, par, h, :], pr[:, par, h, :],
                                          start=False, stop=True, skip_group_check=True)
                mm.then_inc(pv_done, 1)

            def tile_values(n, g):
                if g % NG == 0:
                    pe.wait_ge(vs_ready, JC + 2 * JC * n + g // NG + 1)
                values(STEP_GROUPS * n + g, g)

            def late_values(n, s):
                if (s - LAG) % NG == 0:
                    pe.wait_ge(vs_ready, JC + 2 * JC * n)
                values(STEP_GROUPS * n + s - LAG, STEP_GROUPS + s - LAG)

            def clear_sums(b):
                pe.wait_ge(o_ready, b + 1)
                for i in range(GH):
                    for bank in range(2):
                        nc.tensor.matmul(po[DP * i:DP * (i + 1), 2 * bank:2 * bank + 2, :], zero[:, 0:DP], zero[:, :],
                                         start=True, stop=True, skip_group_check=True)

            def project_out(b):
                pe.wait_ge(o_ready, b + 1)
                pe.wait_ge(k_copied, owed_keys(b))
                for t in range(TB):
                    for g in range(NG):
                        mm = nc.tensor.matmul(pk[:, D * t:D * (t + 1)], oT[:, g, P * t:P * (t + 1)], wo[:, g, :],
                                              start=(g == 0), stop=(g == NG - 1), skip_group_check=True)
                mm.then_inc(proj_ready, 1)

            def owed_keys(b):
                return 1 + MT * (2 * NB * b + (0 if isinstance(b, int) else 2))

            pe.sem_inc(pv_done, PRING)
            pe.wait_ge(wk_in, 32)
            pe.wait_ge(wv_in, 32)
            for k in range(4):
                project(0, 0, 0, 1, k)
            banks = ps[:, :, :, :].rearrange("p b i t -> p b (i t)")
            pe.wait_ge(ident_ready, 2)
            for half in range(2):
                pe.wait_ge(ln_step, LN_INV + 4 * (half + 1))
                turn_half(pe, nc, xn, [banks[:, KT * half + k, :] for k in range(KT)], sb["ident"][:, :], half, turned)
            pe.wait_ge(wq_in, 32)
            pe.wait_ge(turned_out, 4)
            for m in range(MT):
                if m == 1:
                    for k in range(4, 8):
                        project(0, 0, 0, 1, k)
                for half in range(2):
                    for k in range(KT):
                        mm = nc.tensor.matmul(banks[:, 2 * m + half, :], wq[:, k, P * m:P * (m + 1)],
                                              xnT[:, k, 512 * half:512 * (half + 1)],
                                              start=(k == 0), stop=(k == KT - 1))
                    mm.then_inc(q_ready, 1)
            for k in range(8, PRODUCTS):
                project(0, 0, 0, 1, k)
            pe.wait_ge(zeroed, 2)
            pe.wait_ge(k_sent[0], SENT)
            pe.wait_ge(q_step, 5)
            for u in range(2 * AHEAD):
                if u % (H // 2 // MT) == 0:
                    pe.wait_ge(q_sent[u // (H // 2 // MT)], 16 * len(PAIRS))
                scores(u, u, 0, 0)
            pe.wait_ge(q_sent[MT - 1], 16 * len(PAIRS))
            pe.wait_ge(wo_in, 16)
            with pe.Fori(0, B) as b:
                with pe.Fori(0, NB) as it:
                    n = b * NB + it
                    q0 = b * T
                    for s in range(AHEAD, STEP_GROUPS):
                        cc = s // (STEP_GROUPS // 2)
                        if s == STEP_GROUPS // 2:
                            pe.wait_ge(k_sent[1], SENT * (n + 1))
                        for half in range(2):
                            scores(STEP_UNITS * n + 2 * s + half, 2 * s + half, cc, q0)
                        for k in (k for k, slot in SLOT.items() if s % (STEP_GROUPS // 2) - AHEAD == slot):
                            if cc == 0:
                                project(2 * n + 1, 1, n, b + 1, k)
                            else:
                                with pe.If(n < NCH // 2 - 1):
                                    project(2 * n + 2, 0, n + 1, b + 2, k)
                        if s < LAG:
                            with pe.If(it > 0):
                                late_values(n, s)
                        if s == LAG - 1:
                            with pe.If(it < 1):
                                clear_sums(b)
                        if s >= LAG:
                            tile_values(n, s - LAG)
                        if s == STEP_GROUPS // 2 - 2:
                            with pe.If(it < 1):
                                with pe.If(b > 0):
                                    project_out(b)
                    with pe.If(n < NCH // 2 - 1):
                        pe.wait_ge(k_sent[0], SENT * (n + 2))
                    for s in range(STEP_GROUPS, STEP_GROUPS + AHEAD):
                        with pe.If(n < NCH // 2 - 1):
                            for half in range(2):
                                scores(STEP_UNITS * n + 2 * s + half, 2 * (s - STEP_GROUPS) + half, 0,
                                       nc.s_assert_le(((n + 1) // NB) * T, (B - 1) * T))
                        tile_values(n, s - LAG)
                for s in range(AHEAD, LAG):
                    late_values((b + 1) * NB, s)
            project_out(B)

        @block.vector
        def _(dve):
            def copy_keys(m, tile):
                dve.wait_ge(k_ready, tile + 1)
                nc.vector.tensor_scalar(kf[:, m, :], pk[:, :], bk[:, m:m + 1], None, ALU.add).then_inc(k_copied, 1)
                dve.wait_ge(k_copied, tile + 2)
                nc.vector.tensor_copy(kp[:, m, 0, :], kf[:, m, :]).then_inc(k_part0, 1)

            def second_part(m, tile):
                dve.wait_ge(k_rest0, tile + 1)
                nc.vector.tensor_copy(kp[:, m, 1, :], kr[:, m, :]).then_inc(k_part1, 1)

            def copy_values(parity, pair, j2):
                dve.wait_ge(v_ready, j2 + 1)
                nc.vector.tensor_tensor(v[:, parity, 2 * pair:2 * pair + 2, :], pv[:, :, :],
                                        bv[:, :].unsqueeze(1).to_broadcast([P, 2, D]), ALU.add).then_inc(v_copied, 1)

            def maximum(unit, local):
                dve.wait_ge(s_ready, unit + 1)
                jt, hp = divmod(local, H // 2)
                nc.vector.tensor_reduce(nmax[:, jt % 2, 2 * hp:2 * hp + 2], ps[:, local % SRING, :, :], AX.X, ALU.max,
                                        negate=True).then_inc(max_ready, 1)

            def invert(j, local):
                dve.wait_ge(exp_done, SRING + (H // 2) * (j + 1))
                dve.wait_ge(vs_ready, JC + j - 1)
                nc.vector.reciprocal(inv[:, local % 2, :], total[:, local % 2, :]).then_inc(inv_ready, 1)

            def side_work(k, c, parity, sent):
                if k == 2:
                    dve.wait_ge(k_sent[1 - parity], sent)
                if k in (2, 6):
                    copy_keys(k // 6, MT * c + k // 6)
                if k in (4, 9):
                    second_part(k // 9, MT * c + k // 9)
                if k in (7, 13):
                    copy_values(parity, k // 13, JC // 2 * c + k // 13)

            def add_output(b):
                t0 = TB * (b - 1) if isinstance(b, int) else nc.s_assert_within(TB * (b - 1), 0, TB * (B - 1))
                dve.wait_ge(proj_ready, b + 1)
                xt = sb["x"][:, bass.ds(t0, TB), :]
                nc.vector.tensor_tensor(xt, pk[:, :].rearrange("p (t d) -> p t d", d=D), xt, ALU.add)\
                    .then_inc(x_ready, 1)

            def split_queries(m):
                for half in range(2):
                    c = slice(512 * half, 512 * (half + 1))
                    dve.wait_ge(q_ready, 2 * m + half + 1)
                    last = nc.vector.tensor_scalar(qf[:, m, c], ps[:, 2 * m + half, :, :].rearrange("p i t -> p (i t)"),
                                                   bq[:, m:m + 1], DK ** -0.5, ALU.add, ALU.mult)
                last.then_inc(q_step, 1)
                dve.wait_ge(q_step, 4 * m + 1)
                nc.vector.tensor_copy(qp[:, m, 0, :], qf[:, m, :]).then_inc(q_step, 1)
                dve.wait_ge(q_step, 4 * m + 2)
                nc.vector.tensor_tensor(qr[:, m, :], qf[:, m, :], qp[:, m, 0, :], ALU.subtract).then_inc(q_step, 1)
                dve.wait_ge(q_step, 4 * m + 3)
                nc.vector.tensor_copy(qp[:, m, 1, :], qr[:, m, :]).then_inc(q_step, 1)
                dve.wait_ge(q_step, 4 * m + 4)
                nc.vector.tensor_tensor(qp[:, m, 2, :], qr[:, m, :], qp[:, m, 1, :], ALU.subtract).then_inc(q_split, 1)

            dve.sem_inc(o_ready, 1)
            dve.sem_inc(proj_ready, 1)
            dve.sem_inc(k_copied, 1)
            dve.sem_inc(v_copied, 1)
            dve.sem_inc(x_ready, 2)
            dve.wait_ge(x_in, 16)
            layer_norm_vector(dve, nc, sb["x"], xn, stat, 0, TT, ln_step, ln_root)
            dve.wait_ge(wk_in, 32)
            dve.wait_ge(wv_in, 32)
            dve.wait_ge(wq_in, 32)
            for m in range(MT):
                copy_keys(m, m)
                second_part(m, m)
                if m == MT - 1:
                    copy_values(0, 0, 0)
                split_queries(m)
            copy_values(0, 1, 1)
            dve.wait_ge(x_biased, 1)
            for u in range(2 * AHEAD):
                maximum(u, u)
            with dve.Fori(0, B) as b:
                with dve.Fori(0, NB) as it:
                    n = b * NB + it
                    for s in range(AHEAD, STEP_GROUPS):
                        for half in range(2):
                            maximum(STEP_UNITS * n + 2 * s + half, 2 * s + half)
                        if s % NG == 1 and s > NG:
                            invert(2 * JC * n + s // NG - 1, s // NG - 1)
                        k = s % (STEP_GROUPS // 2) - AHEAD
                        if k in (2, 4, 6, 7, 9, 13):
                            if s < STEP_GROUPS // 2:
                                side_work(k, 2 * n + 1, 1, SENT * (n + 1))
                            else:
                                with dve.If(n < NCH // 2 - 1):
                                    side_work(k, 2 * n + 2, 0, SENT * (n + 1))
                        if s == STEP_GROUPS // 2 - 1:
                            with dve.If(it < 1):
                                with dve.If(b > 0):
                                    add_output(b)
                    with dve.If(n < NCH // 2 - 1):
                        for u in range(2 * AHEAD):
                            maximum(STEP_UNITS * (n + 1) + u, u)
                    invert(2 * JC * n + 2 * JC - 1, 2 * JC - 1)
                dve.wait_ge(pv_done, PRING + STEP_GROUPS * NB * (b + 1))
                nc.vector.tensor_copy(oT[:, :, :], po[:, :, :]).then_inc(o_ready, 1)
            dve.wait_ge(x_ready, B + 1)
            layer_norm_vector(dve, nc, sb["x"], sb["xn"], sb["stat"], 0, EARLY, sb["ln2_step"], sb["ln2_root"])
            add_output(B)


def self_attention(nc, dram, sb):
    with ExitStack() as ctx:
        def buf(name, shape, dt=F32):
            return ctx.enter_context(nc.sbuf_tensor(name, shape, dt))

        def sem(name):
            return ctx.enter_context(nc.semaphore(name))

        wqkv, wout, ident = sb["wqkv"], sb["wout"], sb["ident"]
        bout = buf("bout", [P, D])
        logit = buf("logit", [P, 2, HS])
        scale = buf("scale", [P, HS])
        xn, stat, ln_step, ln_root = sb["xn"], sb["stat"], sb["ln2_step"], sb["ln2_root"]
        xnT = buf("sxnT", [P, KT, B * T])
        xbT = buf("sxbT", [P, KT, T])
        qk = buf("qk", [P, TB, 2 * INNER])
        sqr = buf("sqr", [P, 2, 512])
        nst = buf("nst", [P, 4, TB, 2 * HS])
        vv = buf("vv", [P, TB, INNER])
        qkT = buf("qkT", [P, 2 * INNER // P, T])
        nmax = buf("snmax", [P, SR, TB])
        total = buf("stotal", [P, 2, TB])
        inv = buf("sinv", [P, 2, TB])
        pr = buf("spr", [P, 2, TB, T])
        pn = buf("spn", [P, SR, TB, T])
        pT = buf("spT", [P, 2, TB, T])
        aT = buf("aT", [P, INNER // P, T])
        bank = ctx.enter_context(nc.psum_tensor("bank", [P, 8, 512], F32))
        QKV, QT, SC, PT_, OUT = 1, 5, 0, 3, 5
        EARLY_BANKS, LATE_BANKS = (0, 7), (5, 6)
        PROJ = 7

        logit_in, bout_in = sem("logit_in"), sem("bout_in")
        scaled = sem("scaled")
        biased = sem("biased")
        turned, turned_out = sem("sturned"), sem("sturned_out")
        xb_ready = sem("xb_ready")
        norm_step = sem("norm_step")
        root = sem("sroot")
        qkv_ready = sem("qkv_ready")
        squared, qk_copied = sem("squared"), sem("qk_copied")
        summed = sem("summed")
        vv_copied = sem("vv_copied")
        normed = sem("normed")
        qt_ready = sem("qt_ready")
        qt_even, qt_odd = sem("qt_even"), sem("qt_odd")
        s_ready, max_ready, exp_done = sem("ss_ready"), sem("smax_ready"), sem("sexp_done")
        pn_ready, t_ready, t_copied = sem("pn_ready"), sem("t_ready"), sem("t_copied")
        normed_p = sem("normed_p")
        pv_done, o_copied = sem("spv_done"), sem("o_copied")
        out_ready, x_ready = sem("sout_ready"), sem("sx_ready")
        NQK = 2 * INNER // 512 * TB
        NV = INNER // 512 * TB
        NORM_STEPS = 7
        TURNS = [0, 1, 4, 5, 2, 3, 6, 7]
        COLUMNS = [0, 2, 1, 3]

        block = ctx.enter_context(nc.Block())

        @block.sync
        def _(sp):
            sp.dma_start(logit[:, 0, :], dram["logit"]).then_inc(logit_in, 16)
            sp.dma_start(bout[:, :], dram["bout"]).then_inc(bout_in, 16)
            for e in range(E):
                sp.dma_start(sb["fc"][:, e, :, :], dram["fc"][e]).then_inc(sb["fc_in"], 16)

        @block.gpsimd
        def _(pool):
            pool.wait_ge(bout_in, 16)
            pool.wait_ge(ln_step, LN_ALL)
            nc.gpsimd.tensor_tensor(sb["x"][:, :, :], sb["x"][:, :, :],
                                    bout[:, :].unsqueeze(1).to_broadcast([P, TT, D]), ALU.add).then_inc(biased, 1)

        @block.scalar
        def _(act):
            for k in range(KT):
                act.wait_ge(turned, k + 1)
                last = nc.scalar.copy(xbT[:, k, :], bank[:, EARLY_BANKS[k], 0:T])
            last.then_inc(xb_ready, 1)
            layer_norm_root(act, nc, stat, EARLY, TT, ln_step, ln_root, 1)
            copy_half(act, nc, xnT, [bank[:, i, :] for i in EARLY_BANKS], 0, turned, turned_out)
            copy_half(act, nc, xnT, [bank[:, i, :] for i in LATE_BANKS], 1, turned, turned_out)
            act.wait_ge(turned_out, 2 * KT)
            with act.Fori(0, B) as b:
                for m in range(NQK):
                    c, t = divmod(m, TB)
                    act.wait_ge(qkv_ready, (NQK + NV) * b + m + 1)
                    if m >= 2:
                        act.wait_ge(summed, NQK * b + m - 1)
                    nc.scalar.activation(sqr[:, m % 2, :], bank[:, QKV + m % 4, :], ACT.Square).then_inc(squared, 1)
                    nc.scalar.copy(qk[:, t, 512 * c:512 * (c + 1)], bank[:, QKV + m % 4, :]).then_inc(qk_copied, 1)
                act.wait_ge(norm_step, NORM_STEPS * b + 1)
                nc.scalar.activation(nst[:, 1, :, :], nst[:, 0, :, :], ACT.Sqrt).then_inc(root, 1)
                for m in range(NV):
                    c, t = divmod(m, TB)
                    act.wait_ge(qkv_ready, (NQK + NV) * b + NQK + m + 1)
                    nc.scalar.copy(vv[:, t, 512 * c:512 * (c + 1)], bank[:, QKV + (NQK + m) % 4, :])\
                        .then_inc(vv_copied, 1)

                def copy_queries(n):
                    w = TURNS[n]
                    act.wait_ge(qt_ready, NQK * b + n + 1)
                    nc.scalar.copy(qkT[:, 2 * w:2 * w + 2, :],
                                   bank[:, QT + n % 3, :].rearrange("p (a t) -> p a t", a=2)).then_inc(qt_even, 1)

                copy_queries(0)
                copy_queries(2)
                for s in range(HS + TLAG):
                    if s >= TLAG:
                        h = s - TLAG
                        act.wait_ge(t_ready, HS * b + h + 1)
                        if h >= 2:
                            act.wait_ge(pv_done, HS * b + h - 1)
                        nc.scalar.copy(pT[:, h % 2, :, :],
                                       bank[:, PT_ + h % 2, :].rearrange("p (j i) -> p j i", j=TB)).then_inc(t_copied, 1)
                    if s < HS:
                        act.wait_ge(max_ready, HS * b + s + 1)
                        if s >= 2:
                            act.wait_ge(pn_ready, HS * b + s - 1)
                        for i in range(TB):
                            last = nc.scalar.activation(pr[:, s % 2, i, :], bank[:, SC + s % SR, T * i:T * (i + 1)],
                                                        ACT.Exp, bias=nmax[:, s % SR, i:i + 1],
                                                        accum_out=total[:, s % 2, i:i + 1])
                        last.then_inc(exp_done, 1)
                    if s < 2:
                        copy_queries(4 + 2 * s)
                    if s == HS // 2:
                        with act.If(b < B - 1):
                            act.wait_ge(qkv_ready, (NQK + NV) * (b + 1))
                            nc.scalar.copy(xbT[:, :, :], xnT[:, :, bass.ds(nc.s_assert_le(T * (b + 1), T * (B - 1)), T)])\
                                .then_inc(xb_ready, 1)

            layer_norm_root(act, nc, stat, 0, EARLY, sb["ln3_step"], sb["ln3_root"])

        @block.tensor
        def _(pe):
            pe.wait_ge(ln_step, LN_INV + EARLY)
            turn_half(pe, nc, xn, [bank[:, i, :] for i in EARLY_BANKS], ident[:, :], 0, turned)
            pe.wait_ge(sb["attn_in"], 32)

            def project(b, m):
                c, t = divmod(m, TB)
                if m == 0:
                    pe.wait_ge(xb_ready, b + 1)
                if 4 <= m < NQK + 4:
                    pe.wait_ge(qk_copied, NQK * b + m - 3)
                for k in range(KT):
                    mm = nc.tensor.matmul(bank[:, QKV + m % 4, :], xbT[:, k, P * t:P * (t + 1)],
                                          wqkv[:, k, 512 * c:512 * (c + 1)], start=(k == 0), stop=(k == KT - 1))
                mm.then_inc(qkv_ready, 1)

            project(0, 0)
            project(0, 1)
            pe.wait_ge(ln_step, LN_ALL)
            turn_half(pe, nc, xn, [bank[:, i, :] for i in LATE_BANKS], ident[:, :], 1, turned)
            pe.wait_ge(turned_out, 2 * KT)
            with pe.Fori(0, B) as b:
                for m in range(2, NQK + NV):
                    project(b, m)

                def turn_queries(n):
                    w = TURNS[n]
                    pe.wait_ge(normed, NQK * b + 2 * (n // 2) + 2)
                    if n >= 3:
                        pe.wait_ge(qt_even if n % 2 else qt_odd, NQK // 2 * b + (n - 3) // 2 + 1)
                    for a in range(2):
                        for t in range(TB):
                            mm = nc.tensor.transpose(bank[:, QT + n % 3, T * a + P * t:T * a + P * (t + 1)],
                                                     qk[:, t, P * (2 * w + a):P * (2 * w + a + 1)], ident[:, :])
                    mm.then_inc(qt_ready, 1)

                def scores(s):
                    if s >= SR:
                        pe.wait_ge(exp_done, HS * b + s - SR + 1)
                    r = slice(DH * (s % 2), DH * (s % 2 + 1))
                    for i in range(TB):
                        mm = nc.tensor.matmul(bank[:, SC + s % SR, T * i:T * (i + 1)],
                                              qkT[r, s // 2, P * i:P * (i + 1)], qkT[r, HS // 2 + s // 2, :],
                                              start=True, stop=True, skip_group_check=True)
                    mm.then_inc(s_ready, 1)

                for n in range(6):
                    turn_queries(n)
                pe.wait_ge(vv_copied, NV * (b + 1))
                pe.wait_ge(qt_even, NQK // 2 * b + NQK // 4)
                pe.wait_ge(qt_odd, NQK // 2 * b + NQK // 4)
                scores(0)
                turn_queries(6)
                scores(1)
                turn_queries(7)
                scores(2)
                for s in range(HS + TLAG + 1):
                    if TLAG <= s < HS + TLAG:
                        h = s - TLAG
                        pe.wait_ge(pn_ready, HS * b + h + 1)
                        if h >= 2:
                            pe.wait_ge(t_copied, HS * b + h - 1)
                        for j in range(TB):
                            for i in range(TB):
                                mm = nc.tensor.transpose(bank[:, PT_ + h % 2, T * j + P * i:T * j + P * (i + 1)],
                                                         pn[:, h % SR, i, P * j:P * (j + 1)], ident[:, :])
                        mm.then_inc(t_ready, 1)
                    if SR <= s < HS:
                        if s == HS // 2:
                            pe.wait_ge(qt_even, NQK // 2 * (b + 1))
                            pe.wait_ge(qt_odd, NQK // 2 * (b + 1))
                        scores(s)
                    if s > TLAG:
                        h = s - TLAG - 1
                        pe.wait_ge(t_copied, HS * b + h + 1)
                        if h == 0:
                            pe.wait_ge(qt_even, NQK // 2 * (b + 1))
                            pe.wait_ge(qt_odd, NQK // 2 * (b + 1))
                        if h % 2 == 0 and h >= 4:
                            pe.wait_ge(o_copied, HS // 2 * b + h // 2 - 1)
                        for j in range(TB):
                            mm = nc.tensor.matmul(bank[DH * (h % 2):DH * (h % 2 + 1), OUT + h // 2 % 2, 0:T],
                                                  vv[:, j, DH * h:DH * (h + 1)], pT[:, h % 2, j, :],
                                                  start=(j == 0), stop=(j == TB - 1), skip_group_check=True)
                        mm.then_inc(pv_done, 1)
                    if s in (HS + 1, HS + 2):
                        with pe.If(b < B - 1):
                            pe.wait_ge(exp_done, HS * b + s - 2)
                            project(b + 1, s - HS - 1)
                pe.wait_ge(o_copied, HS // 2 * (b + 1))
                for t in range(TB):
                    for k in range(INNER // P):
                        mm = nc.tensor.matmul(bank[:, PROJ, D * t:D * (t + 1)], aT[:, k, P * t:P * (t + 1)],
                                              wout[:, k, :], start=(k == 0), stop=(k == INNER // P - 1),
                                              skip_group_check=True)
                mm.then_inc(out_ready, 1)

        @block.vector
        def _(dve):
            layer_norm_vector(dve, nc, sb["x"], xn, stat, EARLY, TT, ln_step, ln_root, 1)
            dve.wait_ge(logit_in, 16)
            k = 0
            y, t = logit[:, 1, :], scale[:, :]
            steps = [lambda: nc.vector.tensor_scalar(y, logit[:, 0, :], MAX_LOG_SCALE, 1.0 / 64, ALU.min, ALU.mult),
                     lambda: nc.vector.tensor_scalar(t, y, 1.0 / 7, 1.0, ALU.mult, ALU.add)]
            for n in range(6, 0, -1):
                steps.append(lambda: nc.vector.tensor_tensor(t, t, y, ALU.mult))
                steps.append(lambda n=n: nc.vector.tensor_scalar(t, t, 1.0 / n, 1.0, ALU.mult, ALU.add))
            steps += [lambda: nc.vector.tensor_tensor(t, t, t, ALU.mult)] * 6
            for step in steps:
                k += 1
                step().then_inc(scaled, 1)
                dve.wait_ge(scaled, k)
            dve.wait_ge(biased, 1)

            with dve.Fori(0, B) as b:
                for m in range(NQK):
                    c, t = divmod(m, TB)
                    dve.wait_ge(squared, NQK * b + m + 1)
                    nc.vector.tensor_reduce(nst[:, 0, t, 8 * c:8 * (c + 1)],
                                            sqr[:, m % 2, :].rearrange("p (h d) -> p h d", d=DH),
                                            AX.X, ALU.add).then_inc(summed, 1)
                ss, nrm, inn, cor = (nst[:, i, :, :] for i in range(4))
                base = NORM_STEPS * b
                dve.wait_ge(summed, NQK * (b + 1))
                nc.vector.tensor_scalar(ss, ss, NORM_EPS ** 2, None, ALU.max).then_inc(norm_step, 1)
                dve.wait_ge(root, b + 1)
                nc.vector.reciprocal(inn, nrm).then_inc(norm_step, 1)
                dve.wait_ge(norm_step, base + 2)
                nc.vector.tensor_tensor(cor, ss, inn, ALU.mult).then_inc(norm_step, 1)
                dve.wait_ge(norm_step, base + 3)
                nc.vector.tensor_tensor(cor, cor, inn, ALU.mult).then_inc(norm_step, 1)
                dve.wait_ge(norm_step, base + 4)
                nc.vector.tensor_scalar(cor, cor, -0.5, 1.5, ALU.mult, ALU.add).then_inc(norm_step, 1)
                dve.wait_ge(norm_step, base + 5)
                nc.vector.tensor_tensor(inn, inn, cor, ALU.mult).then_inc(norm_step, 1)
                dve.wait_ge(norm_step, base + 6)
                nc.vector.tensor_tensor(inn[:, :, 0:HS], inn[:, :, 0:HS],
                                        scale[:, :].unsqueeze(1).to_broadcast([P, TB, HS]), ALU.mult)\
                    .then_inc(norm_step, 1)
                dve.wait_ge(norm_step, base + 7)
                dve.wait_ge(qk_copied, NQK * (b + 1))

                def normalise(c):
                    for t in range(TB):
                        a = qk[:, t, 512 * c:512 * (c + 1)].rearrange("p (h d) -> p h d", d=DH)
                        nc.vector.tensor_tensor(a, a, inn[:, t, 8 * c:8 * (c + 1)].unsqueeze(2).to_broadcast([P, 8, DH]),
                                                ALU.mult).then_inc(normed, 1)

                def copy_queries(n):
                    w = TURNS[n]
                    dve.wait_ge(qt_ready, NQK * b + n + 1)
                    nc.vector.tensor_copy(qkT[:, 2 * w:2 * w + 2, :],
                                          bank[:, QT + n % 3, :].rearrange("p (a t) -> p a t", a=2)).then_inc(qt_odd, 1)

                normalise(COLUMNS[0])
                normalise(COLUMNS[1])
                normalise(COLUMNS[2])
                copy_queries(1)
                normalise(COLUMNS[3])
                copy_queries(3)
                for s in range(HS + TLAG + 2):
                    if s < HS:
                        dve.wait_ge(s_ready, HS * b + s + 1)
                        nc.vector.tensor_reduce(nmax[:, s % SR, :],
                                                bank[:, SC + s % SR, :].rearrange("p (i j) -> p i j", i=TB),
                                                AX.X, ALU.max, negate=True).then_inc(max_ready, 1)
                    if s < 2:
                        copy_queries(5 + 2 * s)
                    if 1 <= s < HS + 1:
                        h = s - 1
                        dve.wait_ge(exp_done, HS * b + h + 1)
                        if h >= SR:
                            dve.wait_ge(t_ready, HS * b + h - SR + 1)
                        nc.vector.reciprocal(inv[:, h % 2, :], total[:, h % 2, :]).then_inc(normed_p, 1)
                        dve.wait_ge(normed_p, HS * b + h + 1)
                        for i in range(TB):
                            last = nc.vector.tensor_scalar(pn[:, h % SR, i, :], pr[:, h % 2, i, :],
                                                           inv[:, h % 2, i:i + 1], None, ALU.mult)
                        last.then_inc(pn_ready, 1)
                    h = s - TLAG - 2
                    if h >= 0 and h % 2 == 0 and h < HS - 2 or s == HS + TLAG + 1:
                        g = HS // 2 - 1 if s == HS + TLAG + 1 else h // 2
                        dve.wait_ge(pv_done, HS * b + 2 * g + 2)
                        nc.vector.tensor_copy(aT[:, g, :], bank[:, OUT + g % 2, 0:T]).then_inc(o_copied, 1)
                with dve.If(b > B - 2):
                    dve.wait_ge(x_ready, B - 1)
                    layer_norm_vector(dve, nc, sb["x"], xn, stat, 0, EARLY, sb["ln3_step"], sb["ln3_root"])
                dve.wait_ge(out_ready, b + 1)
                x = sb["x"][:, bass.ds(TB * b, TB), :]
                nc.vector.tensor_tensor(x, bank[:, PROJ, :].rearrange("p (t d) -> p t d", d=D), x, ALU.add)\
                    .then_inc(x_ready, 1)


def experts(nc, dram, sb):
    with ExitStack() as ctx:
        def buf(name, shape, dt=F32):
            return ctx.enter_context(nc.sbuf_tensor(name, shape, dt))

        def sem(name):
            return ctx.enter_context(nc.semaphore(name))

        HT = HD // P
        ident, fc = sb["ident"], sb["fc"]
        old = sb["wqkv"][:, :, :].rearrange("p k n -> p (k n)")
        xn, stat, ln_step, root = sb["xn"], sb["stat"], sb["ln3_step"], sb["ln3_root"]
        xnT = old[:, 0:TT * D].rearrange("p (k t) -> p k t", k=KT)
        yg = sb["wout"]
        pj = buf("pj", [P, E, HT, D])
        router = buf("router", [P, KT, E])
        before = buf("before", [P, P])
        ones = buf("ones", [P, P])
        rows = buf("rows", [P, 3, 16])
        upto = buf("upto", [P, E, E])
        lg = buf("lg", [P, TT, E])
        best = buf("best", [P, TT])
        mask = buf("mask", [P, TT, E])
        prior = buf("prior", [P, TT + 1, E])
        cube = buf("cube", [P, E, E])
        tiles = buf("tiles", [P, 3, E])
        pos = buf("pos", [P, TT])
        pos_int = buf("pos_int", [P, TT], mybir.dt.uint32)
        past = buf("past", [P, SLOT_TILES, E])
        expert = buf("expert", [P, SLOT_TILES])
        expert_int = buf("expert_int", [P, SLOT_TILES], mybir.dt.int32)
        xs = buf("xs", [P, 3, D])
        xsT = buf("xsT", [P, 3, KT, P])
        rl = buf("rl", [P, HD])
        hs = buf("hs", [P, HD])
        hT = buf("hT", [P, HT, P])
        y = buf("y", [P, 3, D])
        bank = ctx.enter_context(nc.psum_tensor("ebank", [P, 8, 512], F32))
        HID, HTB, XTB, YB = 0, 2, 4, 5

        const_in, router_in, pj_in = sem("const_in"), sem("router_in"), sem("pj_in")
        turned, turned_out = sem("eturned"), sem("eturned_out")
        lg_ready = sem("lg_ready")
        step = sem("sort_step")
        cum_ready = sem("cum_ready")
        put = sem("put")
        xs_in = [sem(f"xs_in{i}") for i in range(3)]
        xt_ready, xt_copied = sem("ext_ready"), sem("ext_copied")
        h_ready, h_relu, h_square = sem("h_ready"), sem("h_relu"), sem("h_square")
        ht_ready, ht_low = sem("ht_ready"), sem("ht_low")
        ht_high = sem("ht_high")
        y_ready, y_copied = sem("y_ready"), sem("y_copied")
        y_out = [sem(f"y_out{i}") for i in range(3)]
        got = [sem(f"got{b}") for b in range(B)]
        x_ready = sem("ex_ready")
        out_sent = sem("out_sent")
        SORTED, PRIOR = 29, 15
        LAST = SLOT_TILES - 1

        block = ctx.enter_context(nc.Block())

        def tiles_loop(eng, do):
            do(0, 0, True, False)
            with eng.Fori(0, (SLOT_TILES - 1) // 3) as n:
                for i in range(1, 4):
                    do(3 * n + i, i % 3, False, False)
            for t in range(3 * ((SLOT_TILES - 1) // 3) + 1, SLOT_TILES + 1):
                do(t, t % 3, False, t == SLOT_TILES)

        @block.sync
        def _(sp):
            sp.dma_start(before[:, :], dram["before"]).then_inc(const_in, 16)
            sp.dma_start(ones[:, :], dram["ones"]).then_inc(const_in, 16)
            sp.dma_start(rows[:, :, :], dram["rows"]).then_inc(const_in, 16)
            sp.dma_start(upto[:, :, :], dram["upto"]).then_inc(const_in, 16)
            sp.dma_start(router[:, :, :], dram["router"]).then_inc(router_in, 16)
            for e in range(E):
                sp.dma_start(pj[:, e, :, :], dram["pj"][e]).then_inc(pj_in, 16)
            sp.wait_ge(put, 16 * TT)

            def load(t, slot):
                sp.dma_start(xs[:, slot, :], dram["sorted_x"][bass.ds(t, 1), :, :]).then_inc(xs_in[slot], 16)

            for i in range(3):
                load(i, i)

            def store(t, slot):
                sp.wait_ge(y_copied, t + 2)
                sp.dma_start(dram["sorted_y"][bass.ds(t, 1), :, :], y[:, slot, :]).then_inc(y_out[slot], 16)

            for i in range(3):
                sp.sem_inc(y_out[i], 16)
            with sp.Fori(0, SLOT_TILES // 3 - 1) as n:
                for i in range(3):
                    sp.wait_ge(xt_ready, 3 * n + i + 1)
                    load(3 * n + i + 3, i)
                    store(3 * n + i, i)
            for t in range(SLOT_TILES - 3, SLOT_TILES):
                store(t, t % 3)
            for b in range(B):
                sp.wait_ge(x_ready, b + 1)
                sp.dma_start(dram["out"].rearrange("(t p) d -> p t d", p=P)[:, TB * b:TB * (b + 1), :],
                             sb["x"][:, TB * b:TB * (b + 1), :]).then_inc(out_sent, 16)
            sp.wait_ge(out_sent, 16 * B)

        @block.gpsimd
        def _(pool):
            pool.wait_ge(step, SORTED)
            for t in range(TT):
                nc.gpsimd.indirect_dma_start(dram["sorted_x"].rearrange("a p d -> (a p) d"),
                                             bass.IndirectOffsetOnAxis(ap=pos_int[:, t:t + 1], axis=0),
                                             xn[:, t, :], None).then_inc(put, 16)
            for i in range(3):
                pool.wait_ge(y_out[i], 16 * (SLOT_TILES // 3 + 1))
            for t in range(TT):
                nc.gpsimd.indirect_dma_start(yg[:, t, :], None, dram["sorted_y"].rearrange("a p d -> (a p) d"),
                                             bass.IndirectOffsetOnAxis(ap=pos_int[:, t:t + 1], axis=0))\
                    .then_inc(got[t // TB], 16)

        @block.scalar
        def _(act):
            copy_half(act, nc, xnT, [bank[:, k, :] for k in range(KT)], 0, turned, turned_out)
            layer_norm_root(act, nc, stat, EARLY, TT, ln_step, root, 1)
            copy_half(act, nc, xnT, [bank[:, KT + k, :] for k in range(KT)], 1, turned, turned_out)

            def do(t, slot, first, last):
                static = isinstance(t, int)
                if not static or t + 1 <= LAST:
                    act.wait_ge(xt_ready, t + 2)
                    nc.scalar.copy(xsT[:, (slot + 1) % 3, :, :],
                                   bank[:, XTB, 0:D].rearrange("p (k t) -> p k t", k=KT)).then_inc(xt_copied, 1)
                if not first:
                    act.wait_ge(ht_ready, t)
                    nc.scalar.copy(hT[:, 0:HT // 2, :], bank[:, HTB, :].rearrange("p (a t) -> p a t", t=P))\
                        .then_inc(ht_low, 1)
                if not last:
                    act.wait_ge(h_ready, t + 1)
                    nc.scalar.activation(rl[:, :], bank[:, HID:HID + 2, :].rearrange("p a n -> p (a n)"), ACT.Relu)\
                        .then_inc(h_relu, 1)

            act.wait_ge(xt_ready, 1)
            nc.scalar.copy(xsT[:, 0, :, :], bank[:, XTB, 0:D].rearrange("p (k t) -> p k t", k=KT))\
                .then_inc(xt_copied, 1)
            tiles_loop(act, do)

        @block.tensor
        def _(pe):
            pe.wait_ge(ln_step, LN_INV + EARLY)
            pe.wait_ge(router_in, 16)
            for half in range(2):
                if half == 1:
                    pe.wait_ge(ln_step, LN_ALL)
                turn_half(pe, nc, xn, [bank[:, KT * half + k, :] for k in range(KT)], ident[:, :], half, turned)
                pe.wait_ge(turned_out, KT * (half + 1))
                for t in range(4 * half, 4 * half + 4):
                    for k in range(KT):
                        mm = nc.tensor.matmul(bank[:, 7, E * t:E * (t + 1)], xnT[:, k, P * t:P * (t + 1)],
                                              router[:, k, :], start=(k == 0), stop=(k == KT - 1),
                                              skip_group_check=True)
            mm.then_inc(lg_ready, 1)
            pe.wait_ge(const_in, 64)
            pe.wait_ge(step, PRIOR)
            nc.tensor.matmul(bank[:, 6, 0:(TT + 1) * E], ones[:, :], prior[:, :, :].rearrange("p t e -> p (t e)"),
                             start=True, stop=True, skip_group_check=True)
            nc.tensor.matmul(bank[:, 6, 0:TT * E], before[:, :], mask[:, :, :].rearrange("p t e -> p (t e)"),
                             start=False, stop=True, skip_group_check=True).then_inc(cum_ready, 1)

            def turn_rows(t, slot):
                pe.wait_ge(xs_in[slot], 16 * (t // 3 + 1) if isinstance(t, int) else 16 * turn_of(t, slot))
                pe.wait_ge(xt_copied, t)
                for k in range(KT):
                    mm = nc.tensor.transpose(bank[:, XTB, P * k:P * (k + 1)], xs[:, slot, P * k:P * (k + 1)], ident[:, :])
                mm.then_inc(xt_ready, 1)

            def turn_of(t, slot):
                return (t - slot) // 3 + 1

            def do(t, slot, first, last):
                if not first:
                    pe.wait_ge(h_square, t)
                    pe.wait_ge(ht_high, t)
                    for a in range(HT):
                        mm = nc.tensor.transpose(bank[:, HTB + a // 4, P * (a % 4):P * (a % 4 + 1)],
                                                 hs[:, P * a:P * (a + 1)], ident[:, :])
                    mm.then_inc(ht_ready, 1)
                if not isinstance(t, int) or t + 1 <= LAST:
                    turn_rows(t + 1, (slot + 1) % 3)
                if not last:
                    e = pe.value_load(expert_int[0:1, bass.ds(t, 1)], min_val=0, max_val=E)
                    pe.wait_ge(xt_copied, t + 1)
                    with pe.If(e < E):
                        for c in range(2):
                            for k in range(KT):
                                mm = nc.tensor.matmul(bank[:, HID + c, :], xsT[:, slot, k, :],
                                                      fc[:, bass.ds(nc.s_assert_le(e, E - 1), 1), k,
                                                         512 * c:512 * (c + 1)],
                                                      start=(k == 0), stop=(k == KT - 1))
                        mm.then_inc(h_ready, 1)
                    with pe.If(e > E - 1):
                        pe.sem_inc(h_ready, 1)
                if first:
                    pe.wait_ge(pj_in, 16 * E)
                else:
                    e = pe.value_load(expert_int[0:1, bass.ds(t - 1, 1)], min_val=0, max_val=E)
                    pe.wait_ge(ht_low, t)
                    pe.wait_ge(ht_high, t + 1)
                    pe.wait_ge(y_copied, t)
                    with pe.If(e < E):
                        for a in range(HT):
                            mm = nc.tensor.matmul(bank[:, YB, 0:D], hT[:, a, :],
                                                  pj[:, bass.ds(nc.s_assert_le(e, E - 1), 1), a, :],
                                                  start=(a == 0), stop=(a == HT - 1))
                        mm.then_inc(y_ready, 1)
                    with pe.If(e > E - 1):
                        pe.sem_inc(y_ready, 1)

            pe.wait_ge(step, SORTED)
            pe.wait_ge(sb["fc_in"], 16 * E)
            turn_rows(0, 0)
            tiles_loop(pe, do)

        @block.vector
        def _(dve):
            layer_norm_vector(dve, nc, sb["x"], xn, stat, EARLY, TT, ln_step, root, 1)
            dve.wait_ge(lg_ready, 1)
            dve.wait_ge(const_in, 64)
            k = [0]

            def link(ins):
                k[0] += 1
                ins.then_inc(step, 1)
                dve.wait_ge(step, k[0])

            def across(a, shape):
                return a.unsqueeze(1).to_broadcast(shape)

            def along(a, shape):
                return a.unsqueeze(2).to_broadcast(shape)

            te, ee, se = [P, TT, E], [P, E, E], [P, SLOT_TILES, E]
            link(nc.vector.tensor_copy(lg[:, :, :], bank[:, 7, 0:TT * E].rearrange("p (t e) -> p t e", e=E)))
            link(nc.vector.tensor_reduce(best[:, :], lg[:, :, :], AX.X, ALU.max))
            link(nc.vector.tensor_tensor(lg[:, :, :], lg[:, :, :], along(best[:, :], te), ALU.is_equal))
            link(nc.vector.tensor_tensor(lg[:, :, :], lg[:, :, :], across(rows[:, 0, 0:E], te), ALU.mult))
            link(nc.vector.tensor_reduce(best[:, :], lg[:, :, :], AX.X, ALU.max))
            link(nc.vector.tensor_tensor(mask[:, :, :], lg[:, :, :], along(best[:, :], te), ALU.is_equal))
            link(nc.vector.memset(prior[:, 0, :], 0.0))
            for t in range(TT):
                link(nc.vector.tensor_tensor(prior[:, t + 1, :], prior[:, t, :], mask[:, t, :], ALU.add))
            assert k[0] == PRIOR
            dve.wait_ge(cum_ready, 1)
            link(nc.vector.tensor_copy(tiles[:, 0, :], bank[:, 6, TT * E:(TT + 1) * E]))
            link(nc.vector.tensor_tensor(cube[:, :, :], along(tiles[:, 0, :], ee), across(rows[:, 1, 0:E], ee), ALU.is_gt))
            link(nc.vector.tensor_reduce(tiles[:, 0, :], cube[:, :, :], AX.X, ALU.add))
            link(nc.vector.tensor_tensor(cube[:, :, :], across(tiles[:, 0, :], ee), upto[:, :, :], ALU.mult))
            link(nc.vector.tensor_reduce(tiles[:, 1, :], cube[:, :, :], AX.X, ALU.add))
            link(nc.vector.tensor_tensor(tiles[:, 2, :], tiles[:, 1, :], tiles[:, 0, :], ALU.subtract))
            link(nc.vector.tensor_tensor(past[:, :, :], across(tiles[:, 1, :], se),
                                         along(rows[:, 2, 0:SLOT_TILES], se), ALU.is_le))
            link(nc.vector.tensor_reduce(expert[:, :], past[:, :, :], AX.X, ALU.add))
            link(nc.vector.tensor_copy(expert_int[:, :], expert[:, :]))
            link(nc.vector.tensor_scalar(tiles[:, 2, :], tiles[:, 2, :], float(P), None, ALU.mult))
            link(nc.vector.tensor_tensor(lg[:, :, :], bank[:, 6, 0:TT * E].rearrange("p (t e) -> p t e", e=E),
                                         across(tiles[:, 2, :], te), ALU.add))
            link(nc.vector.tensor_tensor(lg[:, :, :], lg[:, :, :], mask[:, :, :], ALU.mult))
            link(nc.vector.tensor_reduce(pos[:, :], lg[:, :, :], AX.X, ALU.add))
            assert k[0] == SORTED - 1
            nc.vector.tensor_copy(pos_int[:, :], pos[:, :]).then_inc(step, 1)

            def do(t, slot, first, last):
                if not first:
                    dve.wait_ge(ht_ready, t)
                    nc.vector.tensor_copy(hT[:, HT // 2:HT, :], bank[:, HTB + 1, :].rearrange("p (a t) -> p a t", t=P))\
                        .then_inc(ht_high, 1)
                if not last:
                    dve.wait_ge(h_relu, t + 1)
                    nc.vector.tensor_tensor(hs[:, :], rl[:, :], rl[:, :], ALU.mult).then_inc(h_square, 1)
                if not first:
                    dve.wait_ge(y_ready, t)
                    dve.wait_ge(y_out[(slot + 2) % 3], 16 * ((t - 1 - (slot + 2) % 3) // 3 + 1))
                    nc.vector.tensor_copy(y[:, (slot + 2) % 3, :], bank[:, YB, 0:D]).then_inc(y_copied, 1)

            dve.sem_inc(ht_high, 1)
            dve.sem_inc(y_copied, 1)
            tiles_loop(dve, do)
            for b in range(B):
                dve.wait_ge(got[b], 16 * TB)
                xb = sb["x"][:, TB * b:TB * (b + 1), :]
                nc.vector.tensor_tensor(xb, xb, yg[:, TB * b:TB * (b + 1), :], ALU.add).then_inc(x_ready, 1)


def program(nc, dram):
    with ExitStack() as ctx:
        def buf(name, shape, dt=F32):
            return ctx.enter_context(nc.sbuf_tensor(name, shape, dt))

        sb = {
            "x": buf("x", [P, TT, D]),
            "ident": buf("ident", [P, P]),
            "xn": buf("xn", [P, TT, D]),
            "stat": buf("stat", [P, TT, 11]),
        }
        for name in ("ln2_step", "ln2_root", "ln3_step", "ln3_root"):
            sb[name] = ctx.enter_context(nc.semaphore(name))
        sb["fc_in"] = ctx.enter_context(nc.semaphore("fc_in"))
        sb["attn_in"] = ctx.enter_context(nc.semaphore("attn_in"))
        with nc.sbuf_tensor("wqkv", [P, KT, 3 * INNER], F32) as sb["wqkv"], \
                nc.sbuf_tensor("wout", [P, INNER // P, D], F32) as sb["wout"]:
            with nc.sbuf_tensor("q_stacked", [KR, H, B * T], BF16) as sb["q"]:
                cross_attention(nc, dram, sb)
            with nc.sbuf_tensor("fc", [P, E, KT, HD], F32) as sb["fc"]:
                self_attention(nc, dram, sb)
                experts(nc, dram, sb)


def kernel(x, ctx_1024, L0_xattn_Wq, L0_xattn_bq, L0_xattn_Wk, L0_xattn_bk, L0_xattn_Wv, L0_xattn_bv, L0_xattn_Wo,
           L0_xattn_bo, L0_attn_w_qkv, L0_attn_w_out, L0_attn_b_out, L0_attn_logit_scale, L0_ffn_router_w,
           L0_ffn_expert_fc, L0_ffn_expert_proj):
    import numpy as np
    import concourse.bacc as bacc
    from concourse.bass_utils import run_bass_kernel_spmd

    def rows(w):
        w = np.asarray(w)
        return w.reshape(w.shape[0] // P, P, -1).transpose(1, 0, 2)

    def by_width(w):
        w = np.asarray(w)
        return w.reshape(-1, MT, HM, DK).transpose(0, 1, 3, 2).reshape(-1, D)

    def every(v):
        return np.broadcast_to(np.asarray(v).reshape(1, -1), (P, np.asarray(v).size))

    wo = np.zeros((NG, GH, DP, D), np.float32)
    wo[:, :, :DK, :] = np.asarray(L0_xattn_Wo).reshape(NG, GH, DK, D)
    lane = np.arange(16, dtype=np.float32)
    arrays = {
        "x": np.asarray(x).reshape(B * T, D),
        "ctxT": np.asarray(ctx_1024).reshape(NCH, CH, KT, P).transpose(0, 3, 2, 1),
        "wq": rows(by_width(L0_xattn_Wq)),
        "bq": by_width(np.asarray(L0_xattn_bq)[None]).reshape(MT, P).T,
        "wk": rows(by_width(L0_xattn_Wk)),
        "bk": by_width(np.asarray(L0_xattn_bk)[None]).reshape(MT, P).T,
        "wv": rows(L0_xattn_Wv),
        "bv": every(L0_xattn_bv),
        "wo": wo.reshape(NG, P, D).transpose(1, 0, 2),
        "bo": every(L0_xattn_bo),
        "wqkv": rows(L0_attn_w_qkv),
        "wout": rows(L0_attn_w_out),
        "bout": every(L0_attn_b_out),
        "logit": every(L0_attn_logit_scale),
        "before": np.triu(np.ones((P, P), np.float32), 1),
        "ones": np.ones((P, P), np.float32),
        "rows": np.broadcast_to(np.stack([E - lane, P * lane, lane]), (P, 3, 16)),
        "upto": np.broadcast_to(np.tril(np.ones((E, E), np.float32)), (P, E, E)),
        "router": rows(np.asarray(L0_ffn_router_w).T),
        "fc": np.asarray(L0_ffn_expert_fc).reshape(E, KT, P, HD).transpose(0, 2, 1, 3),
        "pj": np.asarray(L0_ffn_expert_proj).reshape(E, D, HD // P, P).transpose(0, 3, 2, 1),
    }
    nc = bacc.Bacc("TRN2", target_bir_lowering=False, num_devices=1)
    dram = {}
    for name, a in arrays.items():
        arrays[name] = a = np.ascontiguousarray(a)
        dram[name] = nc.dram_tensor(f"{name}_dram", a.shape, mybir.dt.from_np(a.dtype), kind="ExternalInput").ap()
    for name in ("sorted_x", "sorted_y"):
        dram[name] = nc.dram_tensor(name, (SLOT_TILES, P, D), F32, kind="Internal").ap()
    dram["out"] = nc.dram_tensor("out_dram", (B * T, D), F32, kind="ExternalOutput").ap()
    program(nc, dram)
    r = run_bass_kernel_spmd(nc, [{f"{k}_dram": a for k, a in arrays.items()}], core_ids=[0])
    return r.results[0]["out_dram"].reshape(B, T, D)
```
